# Optimizing a Trainium2 kernel written in Bass

```python
import numpy as np
import jax
import jax.numpy as jnp

def _softmax(x, axis=-1):
    return jax.nn.softmax(x, axis=axis)

def _gelu(x):
    return jax.nn.gelu(x, approximate=True)

def _silu(x):
    return jax.nn.silu(x)

def _sigmoid(x):
    return jax.nn.sigmoid(x)

def _layernorm(x, axis=-1, eps=1e-05):
    m = jnp.mean(x, axis=axis, keepdims=True)
    v = jnp.var(x, axis=axis, keepdims=True)
    return (x - m) / jnp.sqrt(v + eps)

def _scatter_add(tgt, idx, src, axis=0):
    return tgt.at[idx].add(src)

def _segment_sum(src, seg, n):
    return jax.ops.segment_sum(src, seg, n)
kernel_name = 'mk_seq_preln_d1_jaxref_r8_49dbd7'

def setup_inputs(seed: int=0):
    np.random.seed(seed)
    _w = jnp.asarray

    def _L0_attn_setup():
        import jax, jax.numpy as jnp
        import numpy as np
        DIM = 128
        HEADS = 16
        DIM_HEAD = 64
        INNER = HEADS * DIM_HEAD
        EPS = 1e-05

        def layernorm(x, g, b):
            mu = jnp.mean(x, axis=-1, keepdims=True)
            var = jnp.var(x, axis=-1, keepdims=True)
            return (x - mu) * jax.lax.rsqrt(var + EPS) * g + b

        def dynamic_pos_bias(n, pb_w0, pb_b0, pb_ln0_g, pb_ln0_b, pb_w1, pb_b1, pb_ln1_g, pb_ln1_b, pb_w2, pb_b2):
            pos = jnp.arange(-n + 1, n, dtype=jnp.float32)[:, None]
            h = jax.nn.silu(layernorm(pos @ pb_w0 + pb_b0, pb_ln0_g, pb_ln0_b))
            h = jax.nn.silu(layernorm(h @ pb_w1 + pb_b1, pb_ln1_g, pb_ln1_b))
            h = h @ pb_w2 + pb_b2
            i = jnp.arange(n)
            idx = i[:, None] - i[None, :] + (n - 1)
            bias = h[idx]
            return jnp.transpose(bias, (2, 0, 1))

        def attention_fwd(x, ln_g, ln_b, Wq, Wkv, null_kv, null_attn_bias, pb_w0, pb_b0, pb_ln0_g, pb_ln0_b, pb_w1, pb_b1, pb_ln1_g, pb_ln1_b, pb_w2, pb_b2, Wo, out_ln_g, out_ln_b):
            b, n, _ = x.shape
            scale = DIM_HEAD ** (-0.5)
            xn = layernorm(x, ln_g, ln_b)
            q = (xn @ Wq).reshape(b, n, HEADS, DIM_HEAD).transpose(0, 2, 1, 3) * scale
            kv = xn @ Wkv
            k, v = (kv[..., :DIM_HEAD], kv[..., DIM_HEAD:])
            nk = jnp.broadcast_to(null_kv[0], (b, 1, DIM_HEAD))
            nv = jnp.broadcast_to(null_kv[1], (b, 1, DIM_HEAD))
            k = jnp.concatenate([nk, k], axis=1)
            v = jnp.concatenate([nv, v], axis=1)
            sim = jnp.einsum('bhid,bjd->bhij', q, k)
            rel = dynamic_pos_bias(n, pb_w0, pb_b0, pb_ln0_g, pb_ln0_b, pb_w1, pb_b1, pb_ln1_g, pb_ln1_b, pb_w2, pb_b2)
            null_bias = jnp.broadcast_to(null_attn_bias[:, None, None], (HEADS, n, 1))
            attn_bias = jnp.concatenate([null_bias, rel], axis=-1)
            sim = sim + attn_bias[None]
            max_neg = -jnp.finfo(sim.dtype).max
            causal_mask = jnp.triu(jnp.ones((n, n + 1), dtype=bool), k=2)
            sim = jnp.where(causal_mask[None, None], max_neg, sim)
            attn = jax.nn.softmax(sim, axis=-1)
            out = jnp.einsum('bhij,bjd->bhid', attn, v)
            out = out.transpose(0, 2, 1, 3).reshape(b, n, INNER)
            return layernorm(out @ Wo, out_ln_g, out_ln_b)
        key = jax.random.key(seed)
        ks = jax.random.split(key, 16)
        b, n = (2, 256)
        s = 0.02
        inp = {'x': jax.random.normal(ks[0], (b, n, DIM), dtype=jnp.float32), 'ln_g': jnp.ones((DIM,), jnp.float32), 'ln_b': jnp.zeros((DIM,), jnp.float32), 'Wq': jax.random.normal(ks[1], (DIM, INNER), jnp.float32) * s, 'Wkv': jax.random.normal(ks[2], (DIM, 2 * DIM_HEAD), jnp.float32) * s, 'null_kv': jax.random.normal(ks[3], (2, DIM_HEAD), jnp.float32), 'null_attn_bias': jax.random.normal(ks[4], (HEADS,), jnp.float32), 'pb_w0': jax.random.normal(ks[5], (1, DIM), jnp.float32) * s, 'pb_b0': jnp.zeros((DIM,), jnp.float32), 'pb_ln0_g': jnp.ones((DIM,), jnp.float32), 'pb_ln0_b': jnp.zeros((DIM,), jnp.float32), 'pb_w1': jax.random.normal(ks[6], (DIM, DIM), jnp.float32) * s, 'pb_b1': jnp.zeros((DIM,), jnp.float32), 'pb_ln1_g': jnp.ones((DIM,), jnp.float32), 'pb_ln1_b': jnp.zeros((DIM,), jnp.float32), 'pb_w2': jax.random.normal(ks[7], (DIM, HEADS), jnp.float32) * s, 'pb_b2': jnp.zeros((HEADS,), jnp.float32), 'Wo': jax.random.normal(ks[8], (INNER, DIM), jnp.float32) * s, 'out_ln_g': jnp.ones((DIM,), jnp.float32), 'out_ln_b': jnp.zeros((DIM,), jnp.float32)}
        return inp
    _L0_attn_in = _L0_attn_setup()

    def _L0_ffn_setup():
        import jax, jax.numpy as jnp
        import numpy as np
        DIM = 128
        DEPTH = 6
        HEADS = 16
        DIM_HEAD = 64
        WINDOW = 32
        INNER = HEADS * DIM_HEAD
        DIM_INNER = int(DIM * 4 * 2 / 3)
        QK_SCALE = 8.0

        def shift_tokens(t):
            a, s = jnp.split(t, 2, -1)
            s = jnp.pad(s, ((0, 0), (1, 0), (0, 0)))[:, :-1]
            return jnp.concatenate([a, s], -1)

        def l2norm(t):
            return t / jnp.maximum(jnp.linalg.norm(t, axis=-1, keepdims=True), 1e-12)

        def rotate_half(x):
            x1, x2 = jnp.split(x, 2, -1)
            return jnp.concatenate([-x2, x1], -1)

        def rotary_tables(n):
            half = jnp.arange(0, DIM_HEAD, 2, dtype=jnp.float32)
            inv_freq = 1.0 / 10000.0 ** (half / DIM_HEAD)
            t = jnp.arange(n, dtype=jnp.float32)
            freqs = t[:, None] * inv_freq[None, :]
            freqs = jnp.concatenate([freqs, freqs], -1)
            base_scale = (half + 0.4 * DIM_HEAD) / (1.4 * DIM_HEAD)
            power = (t - n // 2) / (WINDOW // 2)
            scale = base_scale[None, :] ** power[:, None]
            scale = jnp.concatenate([scale, scale], -1)
            return (freqs, scale)

        def local_attention(q, k, v):
            b, h, n, d = q.shape
            w = WINDOW
            nw = n // w
            bq = q.reshape(b, h, nw, w, d)
            bk = k.reshape(b, h, nw, w, d)
            bv = v.reshape(b, h, nw, w, d)

            def look(t):
                p = jnp.pad(t, ((0, 0), (0, 0), (1, 0), (0, 0), (0, 0)))
                return jnp.concatenate([p[:, :, :nw], p[:, :, 1:]], axis=3)
            bk2, bv2 = (look(bk), look(bv))
            seq = jnp.arange(n).reshape(nw, w)
            seq_p = jnp.pad(seq, ((1, 0), (0, 0)), constant_values=-1)
            jt = jnp.concatenate([seq_p[:nw], seq_p[1:]], axis=1)
            it = seq[:, :, None]
            jb = jt[:, None, :]
            mask = (it < jb) | (it > jb + w) | (jb == -1)
            sim = jnp.einsum('bhwie,bhwje->bhwij', bq, bk2) * QK_SCALE
            sim = jnp.where(mask, -jnp.finfo(sim.dtype).max, sim)
            attn = jax.nn.softmax(sim, -1)
            out = jnp.einsum('bhwij,bhwje->bhwie', attn, bv2)
            return out.reshape(b, h, n, d)

        def attn_layer(x, Wqkv, qs, ksc, Wo):
            b, n, _ = x.shape
            qkv = x @ Wqkv
            q, k, v = jnp.split(qkv, 3, -1)
            sh = lambda t: t.reshape(b, n, HEADS, DIM_HEAD).transpose(0, 2, 1, 3)
            q, k, v = (sh(q), sh(k), sh(v))
            q = l2norm(q) * qs
            k = l2norm(k) * ksc
            freqs, scale = rotary_tables(n)
            cos, sin = (jnp.cos(freqs), jnp.sin(freqs))
            q = q * cos * scale + rotate_half(q) * sin * scale
            inv = 1.0 / scale
            k = k * cos * inv + rotate_half(k) * sin * inv
            out = local_attention(q, k, v)
            out = out.transpose(0, 2, 1, 3).reshape(b, n, INNER)
            return out @ Wo

        def ffn_layer(x, g, bln, W1, b1, W2, b2):
            mu = x.mean(-1, keepdims=True)
            var = ((x - mu) ** 2).mean(-1, keepdims=True)
            xn = (x - mu) / jnp.sqrt(var + 1e-05) * g + bln
            hg = xn @ W1 + b1
            a, gate = jnp.split(hg, 2, -1)
            return a * jax.nn.gelu(gate, approximate=False) @ W2 + b2
        key = jax.random.key(seed)
        ks = jax.random.split(key, 8)
        B, N = (2, 256)
        init = lambda k, shape: jax.random.normal(k, shape, jnp.float32) * 0.02
        return {'x': jax.random.normal(ks[0], (B, N, DIM), jnp.float32), 'Wqkv': init(ks[1], (DEPTH, DIM, 3 * INNER)), 'q_scale': jnp.ones((DEPTH, DIM_HEAD), jnp.float32), 'k_scale': jnp.ones((DEPTH, DIM_HEAD), jnp.float32), 'Wo': init(ks[2], (DEPTH, INNER, DIM)), 'ln_g': jnp.ones((DEPTH, DIM), jnp.float32), 'ln_b': jnp.zeros((DEPTH, DIM), jnp.float32), 'W1': init(ks[3], (DEPTH, DIM, 2 * DIM_INNER)), 'b1': jnp.zeros((DEPTH, 2 * DIM_INNER), jnp.float32), 'W2': init(ks[4], (DEPTH, DIM_INNER, DIM)), 'b2': jnp.zeros((DEPTH, DIM), jnp.float32)}
    _L0_ffn_in = _L0_ffn_setup()
    _d = {'L0_attn_x': _L0_attn_in['x'], 'L0_attn_ln_g': _L0_attn_in['ln_g'], 'L0_attn_ln_b': _L0_attn_in['ln_b'], 'L0_attn_Wq': _L0_attn_in['Wq'], 'L0_attn_Wkv': _L0_attn_in['Wkv'], 'L0_attn_null_kv': _L0_attn_in['null_kv'], 'L0_attn_null_attn_bias': _L0_attn_in['null_attn_bias'], 'L0_attn_pb_w0': _L0_attn_in['pb_w0'], 'L0_attn_pb_b0': _L0_attn_in['pb_b0'], 'L0_attn_pb_ln0_g': _L0_attn_in['pb_ln0_g'], 'L0_attn_pb_ln0_b': _L0_attn_in['pb_ln0_b'], 'L0_attn_pb_w1': _L0_attn_in['pb_w1'], 'L0_attn_pb_b1': _L0_attn_in['pb_b1'], 'L0_attn_pb_ln1_g': _L0_attn_in['pb_ln1_g'], 'L0_attn_pb_ln1_b': _L0_attn_in['pb_ln1_b'], 'L0_attn_pb_w2': _L0_attn_in['pb_w2'], 'L0_attn_pb_b2': _L0_attn_in['pb_b2'], 'L0_attn_Wo': _L0_attn_in['Wo'], 'L0_attn_out_ln_g': _L0_attn_in['out_ln_g'], 'L0_attn_out_ln_b': _L0_attn_in['out_ln_b'], 'L0_ffn_Wqkv': _L0_ffn_in['Wqkv'], 'L0_ffn_q_scale': _L0_ffn_in['q_scale'], 'L0_ffn_k_scale': _L0_ffn_in['k_scale'], 'L0_ffn_Wo': _L0_ffn_in['Wo'], 'L0_ffn_ln_g': _L0_ffn_in['ln_g'], 'L0_ffn_ln_b': _L0_ffn_in['ln_b'], 'L0_ffn_W1': _L0_ffn_in['W1'], 'L0_ffn_b1': _L0_ffn_in['b1'], 'L0_ffn_W2': _L0_ffn_in['W2'], 'L0_ffn_b2': _L0_ffn_in['b2']}
    _x0 = _d['L0_attn_x']
    _d['L0_attn_x'] = jax.random.normal(jax.random.fold_in(jax.random.key(seed), 1), (4, 512, 128), dtype=_x0.dtype)
    del _x0
    return _d

def reference(L0_attn_x, L0_attn_ln_g, L0_attn_ln_b, L0_attn_Wq, L0_attn_Wkv, L0_attn_null_kv, L0_attn_null_attn_bias, L0_attn_pb_w0, L0_attn_pb_b0, L0_attn_pb_ln0_g, L0_attn_pb_ln0_b, L0_attn_pb_w1, L0_attn_pb_b1, L0_attn_pb_ln1_g, L0_attn_pb_ln1_b, L0_attn_pb_w2, L0_attn_pb_b2, L0_attn_Wo, L0_attn_out_ln_g, L0_attn_out_ln_b, L0_ffn_Wqkv, L0_ffn_q_scale, L0_ffn_k_scale, L0_ffn_Wo, L0_ffn_ln_g, L0_ffn_ln_b, L0_ffn_W1, L0_ffn_b1, L0_ffn_W2, L0_ffn_b2):

    def _L0_attn_ref(x, ln_g, ln_b, Wq, Wkv, null_kv, null_attn_bias, pb_w0, pb_b0, pb_ln0_g, pb_ln0_b, pb_w1, pb_b1, pb_ln1_g, pb_ln1_b, pb_w2, pb_b2, Wo, out_ln_g, out_ln_b):
        import jax, jax.numpy as jnp
        import numpy as np
        DIM = 128
        HEADS = 16
        DIM_HEAD = 64
        INNER = HEADS * DIM_HEAD
        EPS = 1e-05

        def layernorm(x, g, b):
            mu = jnp.mean(x, axis=-1, keepdims=True)
            var = jnp.var(x, axis=-1, keepdims=True)
            return (x - mu) * jax.lax.rsqrt(var + EPS) * g + b

        def dynamic_pos_bias(n, pb_w0, pb_b0, pb_ln0_g, pb_ln0_b, pb_w1, pb_b1, pb_ln1_g, pb_ln1_b, pb_w2, pb_b2):
            pos = jnp.arange(-n + 1, n, dtype=jnp.float32)[:, None]
            h = jax.nn.silu(layernorm(pos @ pb_w0 + pb_b0, pb_ln0_g, pb_ln0_b))
            h = jax.nn.silu(layernorm(h @ pb_w1 + pb_b1, pb_ln1_g, pb_ln1_b))
            h = h @ pb_w2 + pb_b2
            i = jnp.arange(n)
            idx = i[:, None] - i[None, :] + (n - 1)
            bias = h[idx]
            return jnp.transpose(bias, (2, 0, 1))

        def attention_fwd(x, ln_g, ln_b, Wq, Wkv, null_kv, null_attn_bias, pb_w0, pb_b0, pb_ln0_g, pb_ln0_b, pb_w1, pb_b1, pb_ln1_g, pb_ln1_b, pb_w2, pb_b2, Wo, out_ln_g, out_ln_b):
            b, n, _ = x.shape
            scale = DIM_HEAD ** (-0.5)
            xn = layernorm(x, ln_g, ln_b)
            q = (xn @ Wq).reshape(b, n, HEADS, DIM_HEAD).transpose(0, 2, 1, 3) * scale
            kv = xn @ Wkv
            k, v = (kv[..., :DIM_HEAD], kv[..., DIM_HEAD:])
            nk = jnp.broadcast_to(null_kv[0], (b, 1, DIM_HEAD))
            nv = jnp.broadcast_to(null_kv[1], (b, 1, DIM_HEAD))
            k = jnp.concatenate([nk, k], axis=1)
            v = jnp.concatenate([nv, v], axis=1)
            sim = jnp.einsum('bhid,bjd->bhij', q, k)
            rel = dynamic_pos_bias(n, pb_w0, pb_b0, pb_ln0_g, pb_ln0_b, pb_w1, pb_b1, pb_ln1_g, pb_ln1_b, pb_w2, pb_b2)
            null_bias = jnp.broadcast_to(null_attn_bias[:, None, None], (HEADS, n, 1))
            attn_bias = jnp.concatenate([null_bias, rel], axis=-1)
            sim = sim + attn_bias[None]
            max_neg = -jnp.finfo(sim.dtype).max
            causal_mask = jnp.triu(jnp.ones((n, n + 1), dtype=bool), k=2)
            sim = jnp.where(causal_mask[None, None], max_neg, sim)
            attn = jax.nn.softmax(sim, axis=-1)
            out = jnp.einsum('bhij,bjd->bhid', attn, v)
            out = out.transpose(0, 2, 1, 3).reshape(b, n, INNER)
            return layernorm(out @ Wo, out_ln_g, out_ln_b)
        return attention_fwd(x, ln_g, ln_b, Wq, Wkv, null_kv, null_attn_bias, pb_w0, pb_b0, pb_ln0_g, pb_ln0_b, pb_w1, pb_b1, pb_ln1_g, pb_ln1_b, pb_w2, pb_b2, Wo, out_ln_g, out_ln_b)

    def _L0_ffn_ref(x, Wqkv, q_scale, k_scale, Wo, ln_g, ln_b, W1, b1, W2, b2):
        import jax, jax.numpy as jnp
        import numpy as np
        DIM = 128
        DEPTH = 6
        HEADS = 16
        DIM_HEAD = 64
        WINDOW = 32
        INNER = HEADS * DIM_HEAD
        DIM_INNER = int(DIM * 4 * 2 / 3)
        QK_SCALE = 8.0

        def shift_tokens(t):
            a, s = jnp.split(t, 2, -1)
            s = jnp.pad(s, ((0, 0), (1, 0), (0, 0)))[:, :-1]
            return jnp.concatenate([a, s], -1)

        def l2norm(t):
            return t / jnp.maximum(jnp.linalg.norm(t, axis=-1, keepdims=True), 1e-12)

        def rotate_half(x):
            x1, x2 = jnp.split(x, 2, -1)
            return jnp.concatenate([-x2, x1], -1)

        def rotary_tables(n):
            half = jnp.arange(0, DIM_HEAD, 2, dtype=jnp.float32)
            inv_freq = 1.0 / 10000.0 ** (half / DIM_HEAD)
            t = jnp.arange(n, dtype=jnp.float32)
            freqs = t[:, None] * inv_freq[None, :]
            freqs = jnp.concatenate([freqs, freqs], -1)
            base_scale = (half + 0.4 * DIM_HEAD) / (1.4 * DIM_HEAD)
            power = (t - n // 2) / (WINDOW // 2)
            scale = base_scale[None, :] ** power[:, None]
            scale = jnp.concatenate([scale, scale], -1)
            return (freqs, scale)

        def local_attention(q, k, v):
            b, h, n, d = q.shape
            w = WINDOW
            nw = n // w
            bq = q.reshape(b, h, nw, w, d)
            bk = k.reshape(b, h, nw, w, d)
            bv = v.reshape(b, h, nw, w, d)

            def look(t):
                p = jnp.pad(t, ((0, 0), (0, 0), (1, 0), (0, 0), (0, 0)))
                return jnp.concatenate([p[:, :, :nw], p[:, :, 1:]], axis=3)
            bk2, bv2 = (look(bk), look(bv))
            seq = jnp.arange(n).reshape(nw, w)
            seq_p = jnp.pad(seq, ((1, 0), (0, 0)), constant_values=-1)
            jt = jnp.concatenate([seq_p[:nw], seq_p[1:]], axis=1)
            it = seq[:, :, None]
            jb = jt[:, None, :]
            mask = (it < jb) | (it > jb + w) | (jb == -1)
            sim = jnp.einsum('bhwie,bhwje->bhwij', bq, bk2) * QK_SCALE
            sim = jnp.where(mask, -jnp.finfo(sim.dtype).max, sim)
            attn = jax.nn.softmax(sim, -1)
            out = jnp.einsum('bhwij,bhwje->bhwie', attn, bv2)
            return out.reshape(b, h, n, d)

        def attn_layer(x, Wqkv, qs, ksc, Wo):
            b, n, _ = x.shape
            qkv = x @ Wqkv
            q, k, v = jnp.split(qkv, 3, -1)
            sh = lambda t: t.reshape(b, n, HEADS, DIM_HEAD).transpose(0, 2, 1, 3)
            q, k, v = (sh(q), sh(k), sh(v))
            q = l2norm(q) * qs
            k = l2norm(k) * ksc
            freqs, scale = rotary_tables(n)
            cos, sin = (jnp.cos(freqs), jnp.sin(freqs))
            q = q * cos * scale + rotate_half(q) * sin * scale
            inv = 1.0 / scale
            k = k * cos * inv + rotate_half(k) * sin * inv
            out = local_attention(q, k, v)
            out = out.transpose(0, 2, 1, 3).reshape(b, n, INNER)
            return out @ Wo

        def ffn_layer(x, g, bln, W1, b1, W2, b2):
            mu = x.mean(-1, keepdims=True)
            var = ((x - mu) ** 2).mean(-1, keepdims=True)
            xn = (x - mu) / jnp.sqrt(var + 1e-05) * g + bln
            hg = xn @ W1 + b1
            a, gate = jnp.split(hg, 2, -1)
            return a * jax.nn.gelu(gate, approximate=False) @ W2 + b2
        for i in range(DEPTH):
            x = attn_layer(shift_tokens(x), Wqkv[i], q_scale[i], k_scale[i], Wo[i]) + x
            x = ffn_layer(shift_tokens(x), ln_g[i], ln_b[i], W1[i], b1[i], W2[i], b2[i]) + x
        return x
    x = L0_attn_x
    x = x + _L0_attn_ref(_layernorm(x, axis=-1), L0_attn_ln_g, L0_attn_ln_b, L0_attn_Wq, L0_attn_Wkv, L0_attn_null_kv, L0_attn_null_attn_bias, L0_attn_pb_w0, L0_attn_pb_b0, L0_attn_pb_ln0_g, L0_attn_pb_ln0_b, L0_attn_pb_w1, L0_attn_pb_b1, L0_attn_pb_ln1_g, L0_attn_pb_ln1_b, L0_attn_pb_w2, L0_attn_pb_b2, L0_attn_Wo, L0_attn_out_ln_g, L0_attn_out_ln_b)
    x = x + _L0_ffn_ref(_layernorm(x, axis=-1), L0_ffn_Wqkv, L0_ffn_q_scale, L0_ffn_k_scale, L0_ffn_Wo, L0_ffn_ln_g, L0_ffn_ln_b, L0_ffn_W1, L0_ffn_b1, L0_ffn_W2, L0_ffn_b2)
    return x

_drawn_inputs = setup_inputs


def setup_inputs(seed=0):
    import zlib

    import numpy as np

    out = dict(_drawn_inputs(seed))
    spreads = {'L0_attn_ln_g': (1.0, 0.2),
     'L0_attn_ln_b': (0.0, 0.1),
     'L0_attn_pb_b0': (0.0, 1.618),
     'L0_attn_pb_ln0_g': (1.0, 0.6),
     'L0_attn_pb_ln0_b': (0.0, 2.0),
     'L0_attn_pb_b1': (0.0, 0.347),
     'L0_attn_pb_ln1_g': (1.0, 0.6),
     'L0_attn_pb_ln1_b': (0.0, 0.8),
     'L0_attn_pb_b2': (0.0, 0.285),
     'L0_attn_out_ln_g': (1.0, 0.2),
     'L0_attn_out_ln_b': (0.0, 0.1),
     'L0_ffn_q_scale': (1.0, 0.6),
     'L0_ffn_k_scale': (1.0, 0.6),
     'L0_ffn_ln_g': (1.0, 0.6),
     'L0_ffn_ln_b': (0.0, 0.8),
     'L0_ffn_b1': (0.0, 0.8),
     'L0_ffn_b2': (0.0, 0.1)}
    factors = {'L0_ffn_W1': 4.486, 'L0_ffn_W2': 4.334}
    for name, (base, spread) in spreads.items():
        noise = np.random.default_rng([zlib.crc32(name.encode()), seed]).standard_normal(out[name].shape)
        drawn = base * np.exp(spread * noise) if base else spread * noise
        out[name] = jnp.asarray(drawn.astype(out[name].dtype))
    for name, factor in factors.items():
        out[name] = (out[name] * factor).astype(out[name].dtype)
    return out
```

```python
from contextlib import ExitStack

import numpy as np

import concourse.bass as bass
from concourse import mybir

F32 = mybir.dt.float32
BF16 = mybir.dt.bfloat16
I32 = mybir.dt.int32
ALU = mybir.AluOpType
ACT = mybir.ActivationFunctionType
AX = mybir.AxisListType.X

P = 128
NB, NTOK = 4, 512
NT = NTOK // P
TILES = NB * NT
HEADS, DH = 16, 64
PAIRS = HEADS // 2
INNER = HEADS * DH
DEPTH, WIN = 6, 32
NWIN = P // WIN
FF = int(P * 4 * 2 / 3)
FCH = [(0, 128), (128, 128), (256, FF - 256)]
EPS = 1e-5
NEG = -1e30
BATCHES = DEPTH * NB
RSQRT_MAGIC = float(0x5F375A86)
NEWTON = 3

O_QKV = 0
O_WO = O_QKV + 3 * INNER
O_QS = O_WO + PAIRS * P
WSZ = O_QS + 4 * DH
F_W1 = 0
F_W2 = F_W1 + 2 * FF
F_LNG = F_W2 + 3 * P
F_LNB = F_LNG + 1
F_B1 = F_LNB + 1
FSZ = F_B1 + 6
TSZ = NT * 4 * DH


def rotary_base():
    half = np.arange(0, DH, 2, dtype=np.float32)
    inv_freq = (np.float32(1.0) / np.float32(10000.0) ** (half / np.float32(DH))).astype(np.float32)
    t = np.arange(NTOK, dtype=np.float32)
    freqs = (t[:, None] * inv_freq[None, :]).astype(np.float32)
    base = ((half + np.float32(0.4 * DH)) / np.float32(1.4 * DH)).astype(np.float32)
    power = ((t - NTOK // 2) / np.float32(WIN // 2)).astype(np.float32)
    scale = (base[None, :] ** power[:, None]).astype(np.float32)
    cos, sin = np.cos(freqs), np.sin(freqs)
    both = lambda a, b: np.concatenate([a, b], -1)
    qk = np.float32(8.0)
    inv = np.float32(1.0) / scale
    kinds = [both(cos * scale, cos * scale) * qk, both(-sin * scale, sin * scale) * qk,
             both(cos * inv, cos * inv), both(-sin * inv, sin * inv)]
    table = np.stack(kinds, 1).astype(np.float32)
    return np.ascontiguousarray(table.reshape(NT, P, 4, DH).transpose(1, 0, 2, 3))


def window_masks():
    i = np.arange(P)[:, None] % WIN
    j = np.arange(2 * WIN)[None, :]
    inner = (j >= i) & (j <= i + WIN)
    first = inner & ((np.arange(P)[:, None] >= WIN) | (j >= WIN))
    return np.where(np.stack([inner, first], 1), 0.0, NEG).astype(mybir.dt.np(BF16))


def build(nc, a, out):
    ctx = ExitStack()
    with ctx:
        dram = lambda n, s: nc.dram_tensor(n, s, F32, kind="Internal").ap()
        bias_rows = dram("bias_rows", [HEADS, NTOK + P])
        x1_dram = dram("x1_dram", [P, TILES, P])

        def keep(name, shape, dt=F32):
            return ctx.enter_context(nc.sbuf_tensor(name, shape, dt))

        banks = [ctx.enter_context(nc.psum_tensor(f"bank{n}", [P, 512], F32)) for n in range(8)]
        ident = keep("ident", [P, P])
        identb = keep("identb", [P, P], BF16)
        masks = keep("masks", [P, 2, 2 * WIN], BF16)
        y = keep("y", [P, TILES * P])
        W = keep("W", [P, 2 * WSZ])
        WF = keep("WF", [P, FSZ])
        tab = keep("tab", [P, 2 * TSZ])
        tab_base = keep("tab_base", [P, NT, 4, DH])
        ins = dict(a)
        with ExitStack() as front:
            stage_a(nc, front, banks, ins, bias_rows, x1_dram, ident, identb, masks, y, W, WF, tab, tab_base)
        with ExitStack() as back:
            stage_b(nc, back, banks, ins, out, x1_dram, ident, identb, masks, y, W, WF, tab, tab_base)


def wait(eng, sem, value):
    if not isinstance(value, int) or value > 0:
        eng.wait_ge(sem, value)


def wait_apart(eng, passed, sem, value):
    if not isinstance(value, int):
        eng.wait_ge(sem, value).then_inc(passed, 1)
    elif value > 0:
        eng.wait_ge(sem, value)


def layer_of(t, layer):
    return t[layer:layer + 1] if isinstance(layer, int) else t[bass.ds(layer, 1)]


def load_attn(eng, a, W, sem, layer, base):
    def go(o, n, src, split=None):
        dst = W[:, base + o:base + o + n] if isinstance(base, int) else W[:, bass.ds(base + o, n)]
        if split:
            dst = dst.rearrange("p (q n) -> p q n", q=split)
        eng.dma_start(dst, src).then_inc(sem, 16)

    go(O_QKV, 3 * INNER, layer_of(a["L0_ffn_Wqkv"], layer).rearrange("l p n -> (l p) n"))
    go(O_WO, PAIRS * P, layer_of(a["L0_ffn_Wo"], layer).rearrange("l (q p) n -> (l p) q n", p=P), PAIRS)
    h = DH // 2
    for s, name in enumerate(("L0_ffn_q_scale", "L0_ffn_k_scale")):
        src = layer_of(a[name], layer)
        go(O_QS + 2 * s * DH, DH, src.to_broadcast([P, DH]))
        go(O_QS + (2 * s + 1) * DH, h, src[:, h:DH].to_broadcast([P, h]))
        go(O_QS + (2 * s + 1) * DH + h, h, src[:, 0:h].to_broadcast([P, h]))


ATTN_DMAS = 2 + 6


def load_ffn(eng, a, WF, sem, layer):
    def go(o, n, src, rows=P, row0=0):
        eng.dma_start(WF[row0:row0 + rows, o:o + n], src).then_inc(sem, 16)

    go(F_W1, 2 * FF, layer_of(a["L0_ffn_W1"], layer).rearrange("l p n -> (l p) n"))
    for k, (f0, n) in enumerate(FCH):
        go(F_W2 + k * P, P, layer_of(a["L0_ffn_W2"], layer)[:, f0:f0 + n, :].rearrange("l p n -> (l p) n"), n)
    go(F_W2 + 2 * P, P, layer_of(a["L0_ffn_b2"], layer), 1, FCH[2][1])
    go(F_LNG, 1, layer_of(a["L0_ffn_ln_g"], layer).rearrange("l (p o) -> (l p) o", o=1))
    go(F_LNB, 1, layer_of(a["L0_ffn_ln_b"], layer).rearrange("l (p o) -> (l p) o", o=1))
    for s in range(2):
        for k, (f0, n) in enumerate(FCH):
            src = layer_of(a["L0_ffn_b1"], layer)[:, s * FF + f0:s * FF + f0 + n]
            go(F_B1 + 3 * s + k, 1, src.rearrange("l (p o) -> (l p) o", o=1), n)


FFN_DMAS = 1 + 3 + 1 + 2 + 6


def build_tables(pool, tab, tab_base, W, sem, parity):
    def cols(t, o, n):
        return t[:, o:o + n] if isinstance(o, int) else t[:, bass.ds(o, n)]

    dst = cols(tab, parity * TSZ, TSZ).rearrange("p (t k d) -> p t k d", t=NT, k=4)
    qs = cols(W, parity * WSZ + O_QS, 4 * DH).rearrange("p (k d) -> p k d", k=4)
    for t in range(NT):
        last = pool.tensor_tensor(dst[:, t], tab_base[:, t], qs, ALU.mult)
    last.then_inc(sem, 1)


class Chain:

    def __init__(self, eng, sem):
        self.eng, self.sem, self.n = eng, sem, 0

    def __call__(self, ins):
        self.n += 1
        ins.then_inc(self.sem, 1)
        self.eng.wait_ge(self.sem, self.n)


def rsqrt_steps(dve, x, y0, t1, t2):
    steps = [lambda: dve.tensor_scalar(t1.bitcast(I32), x.bitcast(I32), 1, None, ALU.logical_shift_right),
             lambda: dve.tensor_scalar(y0.bitcast(I32), t1.bitcast(I32), -1.0, RSQRT_MAGIC, ALU.mult, ALU.add)]
    for _ in range(NEWTON):
        steps += [lambda: dve.tensor_tensor(t1, y0, y0, ALU.mult),
                  lambda: dve.scalar_tensor_tensor(t2, t1, -0.5, x, ALU.mult, ALU.mult),
                  lambda: dve.scalar_tensor_tensor(y0, t2, 1.5, y0, ALU.add, ALU.mult)]
    return steps


RSQRT_STEPS = 2 + 3 * NEWTON
RN_STEPS = 1 + RSQRT_STEPS
NORM_STEPS = 3 + RSQRT_STEPS + 1


def stage_a(nc, ctx, banks, a, bias_rows, x1_dram, ident, identb, masks, y, W, WF, tab, tab_base):
    def sb(name, shape, dt=F32):
        return ctx.enter_context(nc.sbuf_tensor(name, shape, dt))

    def sem(name):
        return ctx.enter_context(nc.semaphore(name))

    c_ident = nc.inline_tensor(np.eye(P, dtype=np.float32), "c_ident")
    c_identb = nc.inline_tensor(np.eye(P).astype(mybir.dt.np(BF16)), "c_identb")
    c_masks = nc.inline_tensor(window_masks(), "c_masks")
    c_tab = nc.inline_tensor(rotary_base(), "c_tab")
    c_pos = nc.inline_tensor(np.arange(NTOK).reshape(NT, P).T.astype(np.float32).copy(), "c_pos")
    dr = lambda t: t.ap() if hasattr(t, "ap") else t

    setup_only = ExitStack()

    def once(name, shape, dt=F32):
        return setup_only.enter_context(nc.sbuf_tensor(name, shape, dt))

    x = sb("x", [P, TILES, P])
    xn = sb("xn", [P, TILES, P])
    xnT = sb("xnT", [P, TILES * P])
    bias = sb("bias", [P, HEADS, NTOK])
    Wq = sb("Wq", [P, INNER])
    Wk2 = sb("Wk2", [P, 2 * DH])
    Wv = sb("Wv", [P, DH])
    WoA = sb("WoA", [P, PAIRS, P])
    nk_sel = sb("nk_sel", [P, PAIRS, HEADS])
    nv_sel = sb("nv_sel", [P, PAIRS, HEADS])
    Wnull = sb("Wnull", [P, HEADS])
    NvWo = sb("NvWo", [HEADS, P])
    nbias = sb("nbias", [P, HEADS])
    lng = sb("lng", [P, 1])
    lnb = sb("lnb", [P, 1])
    og = sb("og", [P, P])
    ob = sb("ob", [P, P])
    stats = sb("stats", [P, TILES, 6])
    mv = sb("mv", [P, TILES, 2])
    rs = sb("rs", [P, TILES])
    rt = sb("rt", [P, 3, TILES])
    nsn = sb("nsn", [P, TILES, HEADS])
    v = sb("v", [P, TILES, DH])
    WqT = once("WqT", [P, PAIRS, P])
    rows = once("rows", [P, 7, P])
    w1 = once("w1", [P, P])
    w2 = once("w2", [P, HEADS])
    b2c = once("b2c", [HEADS, 1])
    pos = once("pos", [P, NT])
    h = once("h", [P, NT, P])
    h2 = once("h2", [P, NT, P])
    hT = once("hT", [P, NTOK])
    xr = once("xr", [P, TILES * P])
    padded = once("padded", [HEADS, NTOK + P])

    ld = sem("a_loaded")
    ld_w = sem("layer_loaded_first")
    chain = sem("a_dve_chain")
    zero = sem("a_zeroed")
    tr = sem("a_transposed")
    ev = sem("a_evacuated")
    mm = sem("a_product")
    ex = sem("a_exp")
    padded_ok = sem("a_bias_rows_ready")
    h_ok = sem("a_h_affine")
    h_silu = sem("a_h_silu")
    st = sem("a_bias_stored")
    bl = sem("a_bias_loaded")
    tabs = sem("a_tables")
    n_ld = [0]

    with nc.Block() as block:
        bc = lambda t, n: t.rearrange("(o n) -> o n", o=1).to_broadcast([P, n])
        column = lambda t: t.rearrange("(p o) -> p o", o=1)

        @block.sync
        def _(sp):
            def go(dst, src):
                n_ld[0] += 1
                sp.dma_start(dst, src).then_inc(ld, 16)

            go(x[:, :, :], a["L0_attn_x"].rearrange("b (t p) d -> p (b t) d", p=P))
            go(pos[:, :], dr(c_pos))
            go(ident[:, :], dr(c_ident))
            go(identb[:, :], dr(c_identb))
            go(masks[:, :, :], dr(c_masks))
            go(tab_base[:, :, :, :], dr(c_tab))
            for n, name in enumerate(("w0", "b0", "ln0_g", "ln0_b", "b1", "ln1_g", "ln1_b")):
                src = a["L0_attn_pb_" + name]
                go(rows[:, n, :], src.to_broadcast([P, P]) if name == "w0" else bc(src, P))
            go(w1[:, :], a["L0_attn_pb_w1"])
            go(w2[:, :], a["L0_attn_pb_w2"])
            go(b2c[:, :], column(a["L0_attn_pb_b2"]))
            go(lng[:, :], column(a["L0_attn_ln_g"]))
            go(lnb[:, :], column(a["L0_attn_ln_b"]))
            go(og[:, :], bc(a["L0_attn_out_ln_g"], P))
            go(ob[:, :], bc(a["L0_attn_out_ln_b"], P))
            go(Wq[:, :], a["L0_attn_Wq"])
            go(Wk2[:, 0:DH], a["L0_attn_Wkv"][:, 0:DH])
            go(Wk2[:, DH:2 * DH], a["L0_attn_Wkv"][:, 0:DH])
            go(Wv[:, :], a["L0_attn_Wkv"][:, DH:2 * DH])
            go(WoA[:, :, :], a["L0_attn_Wo"].rearrange("(q p) n -> p q n", p=P))
            go(nbias[:, :], bc(a["L0_attn_null_attn_bias"], HEADS))
            sp.wait_ge(zero, 1)
            for which, sel in ((0, nk_sel), (1, nv_sel)):
                for e in range(2):
                    src = a["L0_attn_null_kv"][which:which + 1, :].rearrange("o (d c) -> (o d) c", c=1)
                    for q in range(PAIRS):
                        go(sel[DH * e:DH * e + DH, q, 2 * q + e:2 * q + e + 1], src)
            load_attn(sp, a, W, ld_w, 0, 0)
            load_ffn(sp, a, WF, ld_w, 0)
            sp.wait_ge(padded_ok, 1)
            sp.dma_start(bias_rows, padded[:, :]).then_inc(st, 16)
            sp.wait_ge(st, 16)
            for g in range(4):
                hs = HEADS // 4
                src = bass.AP(tensor=bias_rows.tensor, offset=g * hs * (NTOK + P),
                              ap=[[1, P], [NTOK + P, hs], [1, NTOK]])
                sp.dma_start(bias[:, g * hs:(g + 1) * hs, :], src).then_inc(bl, 16)
            sp.wait_ge(bl, 64)
            sp.wait_ge(ld_w, 16 * (ATTN_DMAS + FFN_DMAS))

        @block.gpsimd
        def _(pool):
            pool.memset(nk_sel[:, :, :], 0.0)
            pool.memset(nv_sel[:, :, :], 0.0).then_inc(zero, 1)
            pool.memset(padded[:, :], NEG).then_inc(zero, 1)
            pool.wait_ge(ld, 16 * n_ld[0])
            pool.wait_ge(ld_w, 16 * (ATTN_DMAS + FFN_DMAS))
            build_tables(pool, tab, tab_base, W, tabs, 0)
            pool.wait_ge(tabs, 1)

        ALL = 16 * n_ld[0]

        @block.vector
        def _(dve):
            dve.wait_ge(ld, ALL)
            step = Chain(dve, chain)

            def norm(dst, src, n, eps=EPS):
                for t in range(n):
                    last = dve.bn_stats(stats[:, t, :], src(t))
                step(last)
                for t in range(n):
                    last = dve.bn_aggr(mv[:, t, :], stats[:, t, :])
                step(last)
                step(dve.tensor_scalar(rt[:, 2, 0:n], mv[:, 0:n, 1], eps, None, ALU.add))
                for s in rsqrt_steps(dve, rt[:, 2, 0:n], rs[:, 0:n], rt[:, 0, 0:n], rt[:, 1, 0:n]):
                    step(s())
                for t in range(n):
                    last = dve.tensor_scalar(dst(t), src(t), mv[:, t, 0:1], rs[:, t:t + 1], ALU.subtract, ALU.mult)
                step(last)

            def affine(dst, g, b):
                row = lambda r: r.unsqueeze(1).broadcast_to([P, NT, P])
                step(dve.tensor_tensor(dst, dst, row(g), ALU.mult))
                dve.tensor_tensor(dst, dst, row(b), ALU.add).then_inc(h_ok, 1)

            norm(lambda t: xn[:, t, :], lambda t: x[:, t, :], TILES)
            norm(lambda t: xn[:, t, :], lambda t: xn[:, t, :], TILES)

            for t in range(NT):
                last = dve.scalar_tensor_tensor(h[:, t, :], rows[:, 0, :], pos[:, t:t + 1], rows[:, 1, :],
                                                ALU.mult, ALU.add)
            step(last)
            for layer in range(2):
                if layer:
                    dve.wait_ge(mm, 1)
                    row = rows[:, 4, :].unsqueeze(1).broadcast_to([P, NT, P])
                    step(dve.tensor_tensor(h[:, :, :], banks[1][:, :].rearrange("p (t n) -> p t n", t=NT), row, ALU.add))
                norm(lambda t: h[:, t, :], lambda t: h[:, t, :], NT)
                affine(h[:, :, :], rows[:, 2 + 3 * layer, :], rows[:, 3 + 3 * layer, :])
                dve.wait_ge(ex, 1 + layer)
                step(dve.tensor_scalar(h2[:, :, :], h2[:, :, :], 1.0, None, ALU.add))
                step(dve.reciprocal(h2[:, :, :], h2[:, :, :]))
                dve.tensor_tensor(h[:, :, :], h[:, :, :], h2[:, :, :], ALU.mult).then_inc(h_silu, 1)
            dve.wait_ge(mm, 2)
            dve.wait_ge(zero, 2)
            dve.tensor_scalar(padded[:, P - 1:P - 1 + NTOK], banks[3][0:HEADS, :], b2c[:, 0:1], None, ALU.add).then_inc(padded_ok, 1)
            dve.wait_ge(mm, 4)
            step(dve.tensor_copy(NvWo[:, :], banks[5][0:HEADS, 0:P]))
            nb = nbias[:, :].unsqueeze(1).broadcast_to([P, TILES, HEADS])
            dve.wait_ge(mm, 5)
            src = banks[6][:, 0:TILES * HEADS].rearrange("p (t n) -> p t n", t=TILES)
            step(dve.tensor_scalar(nsn[:, :, :], src, -float(DH) ** -0.5, None, ALU.mult))
            step(dve.tensor_tensor(nsn[:, :, :], nsn[:, :, :], nb, ALU.subtract))

        @block.scalar
        def _(act):
            act.wait_ge(ld, ALL)
            for b in range(NB):
                act.wait_ge(tr, b + 1)
                act.activation(xr[:, b * NTOK:(b + 1) * NTOK], banks[b % 2][:, ::-1], ACT.Identity,
                               bias=lnb[:, 0:1], scale=lng[:, 0:1])
                act.activation(xnT[:, b * NTOK:(b + 1) * NTOK], banks[b % 2][:, :], ACT.Identity,
                               bias=lnb[:, 0:1], scale=lng[:, 0:1]).then_inc(ev, 1)
            act.wait_ge(tr, 5)
            act.activation(WqT[:, 0:4, :], banks[2][:, :].rearrange("p (q n) -> p q n", q=4), ACT.Copy).then_inc(ev, 1)
            act.wait_ge(tr, 6)
            act.activation(WqT[:, 4:8, :], banks[4][:, :].rearrange("p (q n) -> p q n", q=4), ACT.Copy).then_inc(ev, 1)
            for layer in range(2):
                act.wait_ge(h_ok, 1 + layer)
                act.activation(h2[:, :, :], h[:, :, :], ACT.Exp, scale=-1.0).then_inc(ex, 1)
                act.wait_ge(tr, 7 + layer)
                act.activation(hT[:, :], banks[0][:, :], ACT.Copy).then_inc(ev, 1)
            act.wait_ge(mm, 3)
            act.activation(Wnull[:, :], banks[7][:, 0:HEADS], ACT.Copy).then_inc(ev, 1)
            for g in range(2):
                act.wait_ge(mm, 6 + g)
                act.activation(v[:, 8 * g:8 * g + 8, :], banks[g][:, :].rearrange("p (t n) -> p t n", t=8),
                               ACT.Copy).then_inc(ev, 1)

        @block.tensor
        def _(pe):
            pe.wait_ge(ld, ALL)
            pe.wait_ge(chain, 2 * NORM_STEPS)
            for b in range(NB):
                if b >= 2:
                    pe.wait_ge(ev, b - 1)
                for t in range(NT):
                    last = pe.transpose(banks[b % 2][:, t * P:(t + 1) * P], xn[:, NT * b + t, :], ident[:, :])
                last.then_inc(tr, 1)
            for g, bank in ((0, 2), (1, 4)):
                for q in range(4):
                    w = Wq[:, (4 * g + q) * P:(4 * g + q + 1) * P]
                    last = pe.transpose(banks[bank][:, q * P:(q + 1) * P], w, ident[:, :])
                last.then_inc(tr, 1)
            for layer in range(2):
                pe.wait_ge(h_silu, 1 + layer)
                pe.wait_ge(ev, 4 if not layer else 7)
                for t in range(NT):
                    last = pe.transpose(banks[0][:, t * P:(t + 1) * P], h[:, t, :], ident[:, :])
                last.then_inc(tr, 1)
                pe.wait_ge(ev, 7 + layer)
                if layer == 0:
                    for t in range(NT):
                        last = pe.matmul(banks[1][:, t * P:(t + 1) * P], hT[:, t * P:(t + 1) * P], w1[:, :],
                                         start=True, stop=True)
                else:
                    last = pe.matmul(banks[3][0:HEADS, :], w2[:, :], hT[:, :], start=True, stop=True)
                last.then_inc(mm, 1)
            for q in range(PAIRS):
                last = pe.matmul(banks[7][:, 0:HEADS], WqT[:, q, :], nk_sel[:, q, :], start=q == 0, stop=q == PAIRS - 1)
            last.then_inc(mm, 1)
            for q in range(PAIRS):
                last = pe.matmul(banks[5][0:HEADS, 0:P], nv_sel[:, q, :], WoA[:, q, :], start=q == 0, stop=q == PAIRS - 1)
            last.then_inc(mm, 1)
            pe.wait_ge(ev, 9)
            for t in range(TILES):
                last = pe.matmul(banks[6][:, t * HEADS:(t + 1) * HEADS], xnT[:, t * P:(t + 1) * P], Wnull[:, :],
                                 start=True, stop=True)
            last.then_inc(mm, 1)
            for g in range(2):
                for t in range(8):
                    last = pe.matmul(banks[g][:, t * DH:(t + 1) * DH], xr[:, (8 * g + t) * P:(8 * g + t + 1) * P],
                                     Wv[:, :], start=True, stop=True)
                last.then_inc(mm, 1)

    setup_only.close()
    qT = sb("qT_a", [P, 2, NTOK])
    kT = sb("kT_a", [P, NTOK])
    vb = sb("vb", [P, NT, DH])
    nsb = sb("nsb", [P, NT, HEADS])
    pr = sb("pr", [P, 2, NT, NTOK])
    pT = sb("pT", [P, 2, 1280])
    oT = sb("oT_a", [P, PAIRS, NTOK])
    pn = sb("pn", [P, NT, HEADS])
    pnT = sb("pnT", [HEADS, NTOK])
    negm = sb("negm", [P, 2, NT])
    rsum = sb("rsum", [P, 2, NT])
    rinv = sb("rinv", [P, 2, NT])
    pex = sb("pex", [P, 2, NT])
    att = sb("att", [P, NT, P])
    x1 = sb("x1", [P, NT, P])

    q_mm, k_mm, s_mm, t_mm, o_mm, w_mm, pn_mm = (sem("a_" + n) for n in (
        "q_filled", "k_filled", "scores_filled", "pT_filled", "o_filled", "wo_filled", "pnT_filled"))
    q_ev, k_ev, v_ev, t_ev_act, t_ev_dve, o_ev, pn_ev = (sem("a_" + n) for n in (
        "q_copied", "k_copied", "v_copied", "pT_copied_act", "pT_copied_dve", "o_copied", "pnT_copied"))
    s_sub, p_exp, n_exp, p_norm, small, tail, x1_out, w_read, x1_ok, shifted = (sem("a_" + n) for n in (
        "scores_biased", "p_exp", "null_exp", "p_normed", "row_sums", "tail", "x1_stored",
        "wo_read", "x1_ready", "null_shifted"))
    passed = {e: sem("a_" + e + "_passed_wait") for e in ("dve", "pool")}
    KLEN = [P * (t + 1) for t in range(NT)]
    PT_AT = [0, 512, 896, 1152]
    PT_BANKS = [(0,), (1,), (2, 3)]
    TAIL_STEPS = 2 * NORM_STEPS + 1
    SCORE_BANKS, T_BANKS, O_BANK, Q_BANK = banks[0:4], banks[4:6], banks[6], banks[7]

    with nc.Block() as block:
        @block.sync
        def _(sp):
            with sp.Fori(0, NB) as b:
                wait(sp, x1_ok, b + 1)
                sp.dma_start(x1_dram[:, bass.ds(b * NT, NT), :], x1[:, :, :]).then_inc(x1_out, 16)
            sp.wait_ge(x1_out, 16 * NB)

        @block.gpsimd
        def _(pool):
            with pool.Fori(0, NB) as b:
                pool.wait_ge(o_mm, b * HEADS)
                wait_apart(pool, passed["pool"], shifted, b * HEADS)
                pool.tensor_copy(nsb[:, :, :], nsn[:, bass.ds(b * NT, NT), :])
                pool.tensor_copy(vb[:, :, :], v[:, bass.ds(b * NT, NT), :]).then_inc(v_ev, 1)

        @block.tensor
        def _(pe):
            with pe.Fori(0, NB) as b:
                def q_proj(q):
                    if q == 0:
                        pe.wait_ge(w_read, b)
                    else:
                        pe.wait_ge(q_ev, b * PAIRS + q)
                    pe.matmul(Q_BANK[:, :], Wq[:, q * P:(q + 1) * P], xnT[:, bass.ds(b * NTOK, NTOK)],
                              start=True, stop=True).then_inc(q_mm, 1)

                def scores(n):
                    q, e = divmod(n, 2)
                    rows_ = slice(DH * e, DH * e + DH)
                    pe.wait_ge(q_ev, b * PAIRS + q + 1)
                    for t in range(NT):
                        pe.wait_ge(s_sub, b * HEADS * NT + max(0, (n - 1) * NT + t + 1))
                        pe.matmul(SCORE_BANKS[t][:, 0:KLEN[t]], qT[rows_, q % 2, t * P:(t + 1) * P],
                                  kT[rows_, NTOK - KLEN[t]:NTOK], start=True, stop=True).then_inc(s_mm, 1)

                def turn(n):
                    pe.wait_ge(p_norm, (b * HEADS + n + 1))
                    for g, group in enumerate(PT_BANKS):
                        m = 3 * n + g
                        before, group_before = divmod(m - 2, 3)
                        if before < 0:
                            pe.wait_ge(t_ev_dve, b * 2 * HEADS)
                        elif group_before == 0:
                            pe.wait_ge(t_ev_act, b * HEADS + before + 1)
                        else:
                            pe.wait_ge(t_ev_dve, b * 2 * HEADS + 2 * before + group_before)
                        col = 0
                        for j in group:
                            for t in range(j, NT):
                                last = pe.transpose(T_BANKS[m % 2][:, col:col + P],
                                                    pr[:, n % 2, t, (t - j) * P:(t - j + 1) * P], ident[:, :])
                                col += P
                        last.then_inc(t_mm, 1)

                def product(n):
                    q, e = divmod(n, 2)
                    if n == 0:
                        pe.wait_ge(pn_ev, b)
                    elif e == 0:
                        pe.wait_ge(o_ev, b * PAIRS + q)
                    pe.wait_ge(t_ev_act, b * HEADS + n + 1)
                    pe.wait_ge(t_ev_dve, b * 2 * HEADS + 2 * n + 2)
                    for j in range(NT):
                        last = pe.matmul(O_BANK[DH * e:DH * e + DH, j * P:NTOK], vb[:, NT - 1 - j, :],
                                         pT[:, n % 2, PT_AT[j]:PT_AT[j] + NTOK - j * P],
                                         start=j == 0, stop=j == NT - 1)
                    last.then_inc(o_mm, 1)

                pe.wait_ge(s_sub, b * HEADS * NT)
                pe.matmul(SCORE_BANKS[0][:, :], Wk2[:, :], xnT[:, bass.ds(b * NTOK, NTOK)],
                          start=True, stop=True).then_inc(k_mm, 1)
                q_proj(0)
                pe.wait_ge(k_ev, b + 1)
                pe.wait_ge(v_ev, b + 1)
                for n in range(HEADS + 2):
                    if n < HEADS:
                        scores(n)
                    if n % 2 == 0 and n // 2 + 1 < PAIRS:
                        q_proj(n // 2 + 1)
                    if n >= 2:
                        product(n - 2)
                    if 1 <= n <= HEADS:
                        turn(n - 1)
                pe.wait_ge(o_ev, b * PAIRS + PAIRS)
                for t in range(NT):
                    last = pe.transpose(O_BANK[0:HEADS, t * P:(t + 1) * P], pn[:, t, :], ident[:, :])
                last.then_inc(pn_mm, 1)
                pe.wait_ge(pn_ev, b + 1)
                for t in range(NT):
                    for q in range(PAIRS):
                        pe.matmul(Q_BANK[:, t * P:(t + 1) * P], oT[:, q, t * P:(t + 1) * P], WoA[:, q, :],
                                  start=q == 0, stop=False)
                    last = pe.matmul(Q_BANK[:, t * P:(t + 1) * P], pnT[:, t * P:(t + 1) * P], NvWo[:, :],
                                     start=False, stop=True)
                last.then_inc(w_mm, 1)

        @block.scalar
        def _(act):
            with act.Fori(0, NB) as b:
                def q_copy(q):
                    act.wait_ge(q_mm, b * PAIRS + q + 1)
                    if q >= 2:
                        act.wait_ge(s_mm, b * HEADS * NT + 2 * (q - 1) * NT)
                    act.activation(qT[:, q % 2, :], Q_BANK[:, :], ACT.Copy,
                                   scale=float(DH) ** -0.5).then_inc(q_ev, 1)

                act.wait_ge(k_mm, b + 1)
                act.activation(kT[:, :], SCORE_BANKS[0][:, ::-1], ACT.Copy).then_inc(k_ev, 1)
                q_copy(0)
                for n in range(HEADS + 2):
                    if n < HEADS:
                        for t in range(NT):
                            act.wait_ge(s_sub, b * HEADS * NT + n * NT + t + 1)
                            row = pr[:, n % 2, t, 0:KLEN[t]]
                            last = act.activation(row, row, ACT.Exp, scale=-1.0, bias=negm[:, n % 2, t:t + 1],
                                                  accum_out=rsum[:, n % 2, t:t + 1])
                        last.then_inc(p_exp, 1)
                        act.wait_ge(shifted, b * HEADS + n + 1)
                        act.activation(pex[:, n % 2, :], pex[:, n % 2, :], ACT.Exp).then_inc(n_exp, 1)
                    if n % 2 == 0 and n // 2 + 1 < PAIRS:
                        q_copy(n // 2 + 1)
                    if 1 <= n <= HEADS:
                        m = n - 1
                        act.wait_ge(t_mm, b * 3 * HEADS + 3 * m + 1)
                        if m >= 2:
                            act.wait_ge(o_mm, b * HEADS + m - 1)
                        act.activation(pT[:, m % 2, 0:512], T_BANKS[(3 * m) % 2][:, :], ACT.Copy).then_inc(t_ev_act, 1)
                    if n >= 3 and n % 2 == 1:
                        q = (n - 3) // 2
                        act.wait_ge(o_mm, b * HEADS + 2 * q + 2)
                        act.activation(oT[:, q, :], O_BANK[:, :], ACT.Copy).then_inc(o_ev, 1)
                act.wait_ge(pn_mm, b + 1)
                act.activation(pnT[:, :], O_BANK[0:HEADS, :], ACT.Copy).then_inc(pn_ev, 1)

        @block.vector
        def _(dve):
            with dve.Fori(0, NB) as b:
                def biased(n):
                    for t in range(NT):
                        if t == 0:
                            dve.wait_ge(t_mm, b * 3 * HEADS + max(0, 3 * (n - 1)))
                        wait_apart(dve, passed["dve"], s_mm, b * HEADS * NT + n * NT + t + 1)
                        src = bias[:, n, 0:KLEN[t]]
                        dve.tensor_tensor_reduce(pr[:, n % 2, t, 0:KLEN[t]], SCORE_BANKS[t][:, 0:KLEN[t]], src, -1.0,
                                                 nsb[:, t, n:n + 1], ALU.add, ALU.min,
                                                 negm[:, n % 2, t:t + 1]).then_inc(s_sub, 1)

                def null_shift(n):
                    i = n % 2
                    dve.wait_ge(s_sub, (b * HEADS + n + 1) * NT)
                    dve.tensor_tensor(pex[:, i, :], negm[:, i, :], nsb[:, :, n], ALU.subtract).then_inc(shifted, 1)

                def sums(n):
                    i = n % 2
                    k = 3 * (b * HEADS + n)
                    dve.wait_ge(n_exp, b * HEADS + n + 1)
                    dve.wait_ge(p_exp, b * HEADS + n + 1)
                    dve.tensor_tensor(rsum[:, i, :], rsum[:, i, :], pex[:, i, :], ALU.add).then_inc(small, 1)
                    dve.wait_ge(small, k + 1)
                    dve.reciprocal(rinv[:, i, :], rsum[:, i, :]).then_inc(small, 1)
                    dve.wait_ge(small, k + 2)
                    dve.tensor_tensor(pn[:, :, n], pex[:, i, :], rinv[:, i, :], ALU.mult).then_inc(small, 1)
                    for t in range(NT):
                        row = pr[:, i, t, 0:KLEN[t]]
                        last = dve.tensor_scalar(row, row, rinv[:, i, t:t + 1], None, ALU.mult)
                    last.then_inc(p_norm, 1)

                dve.wait_ge(v_ev, b + 1)
                dve.wait_ge(pn_mm, b)
                for n in range(HEADS + 2):
                    if n < HEADS:
                        biased(n)
                        null_shift(n)
                    if 1 <= n <= HEADS:
                        sums(n - 1)
                    if 1 <= n <= HEADS:
                        m = n - 1
                        if m >= 2:
                            dve.wait_ge(o_mm, b * HEADS + m - 1)
                        for g, at in ((1, 512), (2, 896)):
                            dve.wait_ge(t_mm, b * 3 * HEADS + 3 * m + g + 1)
                            dve.tensor_copy(pT[:, m % 2, at:at + 384],
                                            T_BANKS[(3 * m + g) % 2][:, 0:384]).then_inc(t_ev_dve, 1)
                k = [0]

                def step(ins):
                    k[0] += 1
                    ins.then_inc(tail, 1)
                    wait_apart(dve, passed["dve"], tail, TAIL_STEPS * b + k[0])

                def norm(dst, src, last_of=None):
                    for t in range(NT):
                        last = dve.bn_stats(stats[:, t, :], src(t))
                    step(last)
                    for t in range(NT):
                        last = dve.bn_aggr(mv[:, t, :], stats[:, t, :])
                    step(last)
                    step(dve.tensor_scalar(rt[:, 2, 0:NT], mv[:, 0:NT, 1], EPS, None, ALU.add))
                    for s in rsqrt_steps(dve, rt[:, 2, 0:NT], rs[:, 0:NT], rt[:, 0, 0:NT], rt[:, 1, 0:NT]):
                        step(s())
                    for t in range(NT):
                        last = dve.tensor_scalar(dst(t), src(t), mv[:, t, 0:1], rs[:, t:t + 1],
                                                 ALU.subtract, ALU.mult)
                    if last_of is None:
                        step(last)
                    else:
                        last.then_inc(last_of, 1)
                        dve.wait_ge(last_of, b + 1)

                dve.wait_ge(w_mm, b + 1)
                norm(lambda t: att[:, t, :], lambda t: Q_BANK[:, t * P:(t + 1) * P], w_read)
                row = lambda r: r[:, :].unsqueeze(1).broadcast_to([P, NT, P])
                step(dve.tensor_tensor(att[:, :, :], att[:, :, :], row(og), ALU.mult))
                step(dve.tensor_tensor(att[:, :, :], att[:, :, :], row(ob), ALU.add))
                dve.wait_ge(x1_out, 16 * b)
                dve.tensor_tensor(x1[:, :, :], att[:, :, :], x[:, bass.ds(b * NT, NT), :], ALU.add).then_inc(x1_ok, 1)
                dve.wait_ge(x1_ok, b + 1)
                yb = y[:, bass.ds(b * NTOK, NTOK)]
                norm(lambda t: yb[:, t * P:(t + 1) * P], lambda t: x1[:, t, :])
                assert k[0] == TAIL_STEPS


def stage_b(nc, ctx, banks, a, out, x1_dram, ident, identb, masks, y, W, WF, tab, tab_base):
    def sb(name, shape, dt=F32):
        return ctx.enter_context(nc.sbuf_tensor("b_" + name, shape, dt))

    def sem(name):
        return ctx.enter_context(nc.semaphore("b_" + name))

    yc = sb("yc", [P, 2, P])
    xT = sb("xT", [P, NTOK + 1])
    sq = sb("sq", [P, 4, 512])
    rotA = sb("rotA", [P, 2, 512])
    rotB = sb("rotB", [P, 2, 512])
    qk = sb("qk", [P, 2, 4, 512])
    ssq = sb("ssq", [P, 2, 2 * HEADS])
    rn = sb("rn", [P, NT, 2 * HEADS])
    nt = sb("nt", [P, 2, 2 * HEADS])
    qT = sb("qT", [P, 2, PAIRS, P])
    kT = sb("kT", [P, PAIRS, WIN + NTOK])
    v = sb("v", [P, 2, 2, 512])
    vp = sb("vp", [P, 2, NWIN, 512])
    pr = sb("pr", [P, 2, PAIRS, 2, 2 * WIN])
    pT = sb("pT", [P, PAIRS, P])
    o = sb("o", [P, PAIRS, 2, DH])
    oT = sb("oT", [P, PAIRS, P])
    mx = sb("mx", [P, 2, PAIRS])
    rsum = sb("rsum", [P, 2, PAIRS])
    rinv = sb("rinv", [P, 2, PAIRS])
    xs = sb("xs", [P, NT, P])
    xn = sb("xn", [P, NT, P])
    hT = sb("hT", [P, NTOK])
    gel = sb("gel", [P, 2, 512])
    next_WF = sb("next_WF", [P, FSZ])
    gT = sb("gT", [P, 3, 512])
    stats = sb("stats", [P, NT, 6])
    mv = sb("mv", [P, NT, 2])
    rs = sb("rs", [P, NT])
    rt = sb("rt", [P, 3, NT])
    one = sb("one", [1, 3])

    qk_mm, v_mm, tr_mm, s_mm, pt_mm, o_mm, ot_mm, wo_mm, xn_mm, ga_mm, y2_mm, xt_mm = (
        sem(n + "_filled") for n in ("qk", "v", "qkT", "scores", "pT", "o", "oT", "wo", "xnT", "ffn", "y2", "xT"))
    sq_ev, tr_ev, v_ev, p_exp, pt_ev, ot_ev, xn_ev, ge_ev, xt_ev = (
        sem(n) for n in ("squared", "qkT_copied", "v_copied", "p_exp", "pT_copied", "oT_copied", "hT_copied",
                         "gelu", "xT_copied"))
    tables_in = sem("function_table_loaded")
    rot, ssqd, newt, mxd, subd, sumd, invd, onorm, resid, lnc, gtd, yd = (
        sem(n) for n in ("rot_products", "sums_of_squares", "rsqrt_steps", "row_max", "scores_shifted",
                         "row_sums", "inverse_sums", "o_normed", "attn_added", "ln_steps", "gated", "ffn_added"))
    cleared, added, normd, ycd, tabs = (
        sem(n) for n in ("cleared", "rot_added", "qk_normed", "y_copied", "tables"))
    vp_ld = [sem("vp_loaded_even"), sem("vp_loaded_odd")]
    xs_ld, wa_ld, wf_ld, next_ld = (sem(n) for n in ("xs_loaded", "attn_weights", "ffn_weights", "next_ffn_weights"))
    passed = {e: sem(e + "_passed_wait") for e in ("pe", "dve", "pool", "sp")}
    PJ, TR, SC, OB = banks[0:2], banks[2:4], banks[4:6], banks[6:8]

    def lagged(i, t, lag):
        return i + (t - lag) // NT, (t - lag) % NT

    def live(i, t=0, lag=0):
        i = lagged(i, t, lag)[0]
        return not isinstance(i, int) or 0 <= i < BATCHES

    def cols(tensor, i, size, off, n):
        if isinstance(i, int):
            base = (i // NB) % 2 * size + off
            return tensor[:, base:base + n]
        return tensor[:, bass.ds((i // NB) % 2 * size + off, n)]

    def y_cols(i, off, n, rows=slice(0, P)):
        if isinstance(i, int):
            base = (i % NB) * NTOK + off
            return y[rows, base:base + n]
        return y[rows, bass.ds((i % NB) * NTOK + off, n)]

    def vp_count(i, t):
        return 16 * (18 * i + (8 if t == 0 else 18)) if t % 2 == 0 else 16 * (20 * i + (10 if t == 1 else 20))

    def attn_ready(i):
        return 16 * ATTN_DMAS * (i // NB)

    def pipeline(eng, slot):
        for i in range(2):
            for t in range(NT):
                slot(i, t)
        with eng.Fori(2, BATCHES - 1) as i:
            for t in range(NT):
                slot(i, t)
        for i in range(BATCHES - 1, BATCHES + 2):
            for t in range(NT):
                slot(i, t)

    with nc.Block() as block:
        @block.tensor
        def _(pe):
            pe.wait_ge(cleared, 1)

            def turn_x(i, t):
                g = NT * i + t
                wait(pe, ycd, g + 1)
                pe.transpose(PJ[1][:, 0:P], yc[:, t % 2, :], ident[:, :]).then_inc(xt_mm, 1)

            def project(i, t, j):
                g = NT * i + t
                if j == 0:
                    wait(pe, xt_ev, g + 1)
                    if t == 0:
                        wait(pe, wa_ld, attn_ready(i))
                    if isinstance(i, int):
                        wait(pe, rot, 4 * g - 1)
                        wait(pe, v_ev, 2 * (g - 3) + 1)
                    wait(pe, resid, g - 4)
                if j == 1:
                    if t == 1 and live(i - 2):
                        wait(pe, xn_ev, i - 1)
                    if t == 0 and live(i - 3):
                        wait(pe, yd, i - 2)
                if j >= 2:
                    pe.wait_ge(rot, 4 * g + j - 1)
                pe.matmul(PJ[j % 2][:, :], xT[:, t * P:(t + 1) * P], cols(W, i, WSZ, O_QKV + 512 * j, 512),
                          start=True, stop=True).then_inc(qk_mm, 1)

            def turn_qk(i, t, j):
                g = NT * i + t
                pe.wait_ge(normd, 4 * g + j + 1)
                if j < 2:
                    if isinstance(i, int):
                        wait(pe, tr_ev, 4 * g + j - 1)
                        wait(pe, pt_ev, 2 * (g - 3) + j + 1)
                    wait(pe, ot_ev, 2 * (g - 4) + j + 1)
                else:
                    pe.wait_ge(tr_ev, 4 * g + j - 1)
                for q in range(4):
                    last = pe.transpose(TR[j % 2][:, q * P:(q + 1) * P], qk[:, t % 2, j, q * P:(q + 1) * P],
                                        ident[:, :])
                last.then_inc(tr_mm, 1)

            def turn_p(i, t, j, fed):
                g = NT * i + t
                wait(pe, p_exp, 2 * g + 2)
                if fed:
                    wait(pe, tr_ev, 4 * (g + 2) + j + 3)
                else:
                    wait(pe, ot_ev, 2 * (g - 2) + j + 1)
                for q in range(4):
                    last = pe.transpose(TR[j][:, q * P:(q + 1) * P],
                                        pr[:, t % 2, 4 * j + q, :, :].rearrange("p e k -> p (e k)"), ident[:, :])
                last.then_inc(pt_mm, 1)

            def turn_o(i, t, j, fed):
                g = NT * i + t
                wait(pe, onorm, 2 * g + 2)
                if fed:
                    wait(pe, pt_ev, 2 * (g + 1) + j + 1)
                else:
                    wait(pe, ot_ev, 2 * (g - 1) + j + 1)
                for q in range(4):
                    last = pe.transpose(TR[j][:, q * P:(q + 1) * P],
                                        o[:, 4 * j + q, :, :].rearrange("p e d -> p (e d)"), ident[:, :])
                last.then_inc(ot_mm, 1)

            def project_v(i, t, j, fed, before):
                g = NT * i + t
                if fed:
                    wait(pe, rot, 4 * (g + 2) + j + 3)
                else:
                    wait(pe, v_ev, 2 * (g - 1) + j + 1)
                    for s, value in before:
                        wait(pe, s, value)
                w = cols(W, i, WSZ, O_QKV + 2 * INNER, INNER).rearrange("p (q e d) -> p e q d", e=2, d=DH)
                pe.matmul(PJ[j][:, :].rearrange("p (q d) -> p q d", d=DH), xT[:, t * P:(t + 1) * P], w[:, j],
                          start=True, stop=True).then_inc(v_mm, 1)

            def mask_scores(i, t):
                g = NT * i + t
                pe.wait_ge(tr_ev, 4 * g + 4)
                wait(pe, subd, 2 * g)
                m = masks[:, 1 if t == 0 else 0, :].unsqueeze(1).broadcast_to([P, PAIRS, 2 * WIN])
                for e in range(2):
                    pe.matmul(SC[e][:, :].rearrange("p (q k) -> p q k", q=PAIRS), identb[:, :], m,
                              start=True, stop=False, skip_group_check=True)

            def scores(i, t, w):
                rows = slice(WIN * w, WIN * w + WIN)
                at = t * P + w * WIN
                for q in range(PAIRS):
                    for e in range(2):
                        half = slice(DH * e, DH * e + DH)
                        last = pe.matmul(SC[e][rows, q * 2 * WIN:(q + 1) * 2 * WIN], qT[half, t % 2, q, rows],
                                         kT[half, q, at:at + 2 * WIN], start=False, stop=True,
                                         skip_group_check=True)
                if w == NWIN - 1:
                    last.then_inc(s_mm, 1)

            def product(i, t):
                g = NT * i + t
                pe.wait_ge(pt_ev, 2 * g + 2)
                wait_apart(pe, passed["pe"], vp_ld[t % 2], vp_count(i, t))
                for w in range(NWIN):
                    rows = slice(WIN * w, WIN * w + WIN)
                    for q in range(PAIRS):
                        for e in range(2):
                            half = slice(DH * e, DH * e + DH)
                            last = pe.matmul(OB[e][rows, q * DH:(q + 1) * DH], pT[half, q, rows],
                                             vp[half, t % 2, w, q * DH:(q + 1) * DH], start=True, stop=True)
                last.then_inc(o_mm, 1)

            def project_o(i, t):
                g = NT * i + t
                pe.wait_ge(ot_ev, 2 * g + 2)
                w = cols(W, i, WSZ, O_WO, PAIRS * P)
                for q in range(PAIRS):
                    last = pe.matmul(PJ[0][:, 0:P], oT[:, q, :], w[:, q * P:(q + 1) * P],
                                     start=q == 0, stop=q == PAIRS - 1)
                last.then_inc(wo_mm, 1)

            def turn_xn(i):
                pe.wait_ge(lnc, NORM_STEPS * i + NORM_STEPS)
                for t in range(NT):
                    last = pe.transpose(PJ[1][:, t * P:(t + 1) * P], xn[:, t, :], ident[:, :])
                last.then_inc(xn_mm, 1)

            def expand(i, k):
                n = FCH[k][1]
                pe.wait_ge(xn_ev, i + 1)
                if k == 0:
                    wait(pe, wf_ld, 16 * (i // NB))
                for s, bank in ((1, OB[0]), (0, OB[1])):
                    c = F_W1 + s * FF + FCH[k][0]
                    last = pe.matmul(bank[0:n, :], WF[:, c:c + n], hT[:, :], start=True, stop=True)
                last.then_inc(ga_mm, 1)

            def contract(i):
                pe.wait_ge(gtd, 3 * i + 3)
                for t in range(NT):
                    for k, (_, n) in enumerate(FCH):
                        n += k == 2
                        last = pe.matmul(PJ[1][:, t * P:(t + 1) * P], gT[0:n, k, t * P:(t + 1) * P],
                                         WF[0:n, F_W2 + k * P:F_W2 + (k + 1) * P], start=k == 0, stop=k == 2)
                last.then_inc(y2_mm, 1)

            turn_x(0, 0)

            def slot(i, t):
                g = NT * i + t
                fed = live(i)
                ffn = live(i - 2)
                if live(i, t, 2):
                    mask_scores(*lagged(i, t, 2))
                for j in range(4):
                    if live(i, t, 2):
                        scores(*lagged(i, t, 2), j)
                    if fed:
                        project(i, t, j)
                    if ffn and t == 1 and j == 0:
                        if fed:
                            pe.wait_ge(xt_ev, g + 1)
                        elif live(i, t, 3):
                            pe.wait_ge(v_ev, 2 * (g - 3) + 2)
                        else:
                            pe.wait_ge(yd, i - 2)
                        turn_xn(i - 2)
                    if live(i, t, 1):
                        turn_qk(*lagged(i, t, 1), j)
                    if j == 1 and ffn and t >= 1:
                        if live(i, t, 4):
                            wait(pe, onorm, 2 * (g - 4) + 2)
                        wait(pe, gtd, 3 * (i - 2) + t - 1)
                        expand(i - 2, t - 1)
                before = [(resid, g - 4)], [(xn_ev, i - 1)] if t == 1 else [(yd, i - 2)] if t == 0 else []
                for j in range(2):
                    if live(i, t, 3):
                        turn_p(*lagged(i, t, 3), j, live(i, t, 1))
                    if live(i, t, 2):
                        project_v(*lagged(i, t, 2), j, fed, before[j])
                if live(i, t, 4):
                    for j in range(2):
                        turn_o(*lagged(i, t, 4), j, live(i, t, 3))
                if live(i, t, -1):
                    if live(i, t, 2):
                        wait(pe, v_ev, 2 * (g - 2) + 2)
                    else:
                        wait(pe, rot, 4 * g + 4)
                    turn_x(*lagged(i, t, -1))
                if live(i, t, 3):
                    if ffn and t >= 1:
                        wait(pe, gtd, 3 * (i - 2) + t)
                    if t == 0 and live(i - 3):
                        wait(pe, gtd, 3 * (i - 3) + 3)
                    wait(pe, onorm, 2 * (g - 4) + 2)
                    product(*lagged(i, t, 3))
                if live(i, t, 4):
                    if live(i, t, 2):
                        wait(pe, v_ev, 2 * (g - 2) + 1)
                    else:
                        wait(pe, resid, g - 4)
                    project_o(*lagged(i, t, 4))
                if ffn and t == 3:
                    if live(i, t, -1):
                        pe.wait_ge(xt_ev, g + 2)
                    elif live(i, t, 2):
                        pe.wait_ge(v_ev, 2 * (g - 2) + 2)
                    else:
                        pe.wait_ge(xn_ev, i - 1)
                    contract(i - 2)

            pipeline(pe, slot)

        @block.scalar
        def _(act):
            act.wait_ge(cleared, 1)

            def copy_x(i, t):
                act.wait_ge(xt_mm, NT * i + t + 1)
                act.activation(xT[0:DH, t * P:(t + 1) * P], PJ[1][0:DH, 0:P], ACT.Copy)
                act.activation(xT[DH:P, t * P + 1:(t + 1) * P + 1], PJ[1][DH:P, 0:P], ACT.Copy).then_inc(xt_ev, 1)

            def square(i, t, j):
                g = NT * i + t
                act.wait_ge(qk_mm, 4 * g + j + 1)
                wait(act, ssqd, 2 * g - 1 + j // 2)
                act.activation(sq[:, j, :], PJ[j % 2][:, :], ACT.Square).then_inc(sq_ev, 1)

            def copy_qk(i, t, j):
                g = NT * i + t
                act.wait_ge(tr_mm, 4 * g + j + 1)
                if j == 0:
                    wait(act, s_mm, g - 1)
                src = TR[j % 2][:, :].rearrange("p (q n) -> p q n", q=4)
                q = 4 * (j % 2)
                if j < 2:
                    dst = qT[:, t % 2, q:q + 4, :]
                else:
                    dst = kT[:, q:q + 4, WIN + t * P:WIN + (t + 1) * P]
                act.activation(dst, src, ACT.Copy).then_inc(tr_ev, 1)

            def copy_p(i, t, j):
                g = NT * i + t
                act.wait_ge(pt_mm, 2 * g + j + 1)
                wait(act, o_mm, g)
                act.activation(pT[:, 4 * j:4 * j + 4, :], TR[j][:, :].rearrange("p (q n) -> p q n", q=4),
                               ACT.Copy).then_inc(pt_ev, 1)

            def copy_v(i, t, j):
                g = NT * i + t
                act.wait_ge(v_mm, 2 * g + j + 1)
                for back in (1, 2):
                    if live(i, t, back):
                        act.wait_ge(vp_ld[(t - back) % 2], vp_count(*lagged(i, t, back)))
                act.activation(v[:, t % 2, j, :], PJ[j][:, :], ACT.Copy).then_inc(v_ev, 1)

            def copy_o(i, t, j):
                g = NT * i + t
                act.wait_ge(ot_mm, 2 * g + j + 1)
                wait(act, wo_mm, g)
                act.activation(oT[:, 4 * j:4 * j + 4, :], TR[j][:, :].rearrange("p (q n) -> p q n", q=4),
                               ACT.Copy).then_inc(ot_ev, 1)

            def exponentials(i, t, e):
                g = NT * i + t
                act.wait_ge(subd, 2 * g + e + 1)
                row = pr[:, t % 2, :, e, :]
                act.activation(row, row, ACT.Exp).then_inc(p_exp, 1)

            def gelu(i, k):
                n = FCH[k][1]
                act.wait_ge(ga_mm, 3 * i + k + 1)
                wait(act, gtd, 3 * i + (k == 2))
                act.activation(gel[0:n, k % 2, :], OB[0][0:n, :], ACT.Gelu,
                               bias=WF[0:n, F_B1 + 3 + k:F_B1 + 4 + k]).then_inc(ge_ev, 1)

            def copy_xn(i):
                wait(act, wf_ld, 16 * (i // NB))
                act.wait_ge(xn_mm, i + 1)
                act.activation(hT[:, :], PJ[1][:, :], ACT.Identity, scale=WF[:, F_LNG:F_LNG + 1],
                               bias=WF[:, F_LNB:F_LNB + 1]).then_inc(xn_ev, 1)

            def load_table(n, kind):
                wait(act, tables_in, 2 * n + kind)
                act.activation(one[:, 1 + kind:2 + kind], one[:, 0:1],
                               ACT.Exp if kind else ACT.Gelu).then_inc(tables_in, 1)

            copy_x(0, 0)

            def slot(i, t):
                for j in range(4):
                    if live(i):
                        square(i, t, j)
                    if j == 0 and live(i - 2) and t == 1:
                        copy_xn(i - 2)
                    if live(i, t, 1):
                        copy_qk(*lagged(i, t, 1), j)
                    if j == 2 and live(i - 2) and t >= 1:
                        gelu(i - 2, t - 1)
                for j in range(2):
                    if live(i, t, 3):
                        copy_p(*lagged(i, t, 3), j)
                    if live(i, t, 2):
                        copy_v(*lagged(i, t, 2), j)
                if live(i, t, 4):
                    for j in range(2):
                        copy_o(*lagged(i, t, 4), j)
                if live(i, t, -1):
                    copy_x(*lagged(i, t, -1))
                if live(i - 2) and t >= 1:
                    load_table(3 * (i - 2) + t - 1, 1)
                if live(i, t, 2):
                    for e in range(2):
                        exponentials(*lagged(i, t, 2), e)
                if live(i - 2 + (t + 1) // NT) and t < 3 and live(i - 2):
                    load_table(3 * (i - 2) + t, 0)
            pipeline(act, slot)

        @block.vector
        def _(dve):
            def rotate(i, t, j):
                g = NT * i + t
                dve.wait_ge(sq_ev, 4 * g + j + 1)
                wait(dve, added, 4 * g + j - 1)
                kind = 2 * (j // 2)
                table = lambda k: cols(tab, i, TSZ, (4 * t + k) * DH, DH)
                bank = PJ[j % 2][:, :]
                dve.tensor_tensor(rotA[:, j % 2, :].rearrange("p (h d) -> p h d", d=DH),
                                  bank.rearrange("p (h d) -> p h d", d=DH),
                                  table(kind).unsqueeze(1).broadcast_to([P, 8, DH]), ALU.mult)
                swapped = bank.rearrange("p (h s d) -> p h s d", h=8, s=2)[:, :, ::-1, :]
                sin = table(kind + 1).rearrange("p (s d) -> p s d", s=2).unsqueeze(1).broadcast_to([P, 8, 2, DH // 2])
                dve.tensor_tensor(rotB[:, j % 2, :].rearrange("p (h s d) -> p h s d", h=8, s=2),
                                  swapped, sin, ALU.mult).then_inc(rot, 1)

            def sum_squares(i, t, part):
                g = NT * i + t
                if part == 0:
                    wait(dve, newt, RN_STEPS * (g - 1))
                dve.tensor_reduce(ssq[:, t % 2, HEADS * part:HEADS * (part + 1)],
                                  sq[:, 2 * part:2 * part + 2, :].rearrange("p j (h d) -> p (j h) d", d=DH),
                                  AX, ALU.add).then_inc(ssqd, 1)

            def inverse_norms(i, t):
                g = NT * i + t
                s = ssq[:, t % 2, :]
                dve.wait_ge(ssqd, 2 * g + 2)
                steps = [lambda: dve.tensor_scalar(s, s, 1e-24, None, ALU.max)]
                steps += rsqrt_steps(dve, s, rn[:, t, :], nt[:, 0, :], nt[:, 1, :])
                assert len(steps) == RN_STEPS
                return steps

            def side_by_side(i, t):
                g = NT * i + t
                one = inverse_norms(i, t) if live(i) else []
                two = layernorm(i - 2) if live(i - 2) and t == 0 else []
                for k in range(max(len(one), len(two))):
                    if k < len(one):
                        one[k]().then_inc(newt, 1)
                    if k < len(two):
                        two[k]().then_inc(lnc, 1)
                    if k < len(one):
                        dve.wait_ge(newt, RN_STEPS * g + k + 1)
                    if k < len(two):
                        wait_apart(dve, passed["dve"], lnc, NORM_STEPS * (i - 2) + k + 1)

            def shift(i, t):
                g = NT * i + t
                dve.wait_ge(s_mm, g + 1)
                wait(dve, pt_mm, 2 * (g - 1))
                for e in range(2):
                    s = SC[e][:, :].rearrange("p (q k) -> p q k", q=PAIRS)
                    dve.tensor_reduce(mx[:, e, :], s, AX, ALU.max).then_inc(mxd, 1)
                for e in range(2):
                    s = SC[e][:, :].rearrange("p (q k) -> p q k", q=PAIRS)
                    dve.wait_ge(mxd, 2 * g + e + 1)
                    dve.tensor_tensor(pr[:, t % 2, :, e, :], s,
                                      mx[:, e, :].unsqueeze(2).broadcast_to([P, PAIRS, 2 * WIN]),
                                      ALU.subtract).then_inc(subd, 1)

            def row_sums(i, t):
                g = NT * i + t
                for e in range(2):
                    dve.wait_ge(p_exp, 2 * g + e + 1)
                    dve.tensor_reduce(rsum[:, e, :], pr[:, t % 2, :, e, :], AX, ALU.add).then_inc(sumd, 1)
                dve.wait_ge(sumd, 2 * g + 2)
                dve.reciprocal(rinv[:, :, :], rsum[:, :, :]).then_inc(invd, 1)

            def normalize_o(i, t):
                g = NT * i + t
                dve.wait_ge(o_mm, g + 1)
                dve.wait_ge(invd, g + 1)
                wait(dve, ot_mm, 2 * g)
                for e in range(2):
                    dve.tensor_tensor(o[:, :, e, :], OB[e][:, :].rearrange("p (q d) -> p q d", d=DH),
                                      rinv[:, e, :].unsqueeze(2).broadcast_to([P, PAIRS, DH]),
                                      ALU.mult).then_inc(onorm, 1)

            def add_attention(i, t):
                g = NT * i + t
                dve.wait_ge(wo_mm, g + 1)
                rows = y_cols(i, t * P, P)
                dve.tensor_tensor(rows, PJ[0][:, 0:P], rows, ALU.add).then_inc(resid, 1)

            def layernorm(i):
                dve.wait_ge(xs_ld, 48 * i + 48)
                wait(dve, xn_mm, i)

                def tiles(make):
                    for t in range(NT):
                        last = make(t)
                    return last

                steps = [lambda: tiles(lambda t: dve.bn_stats(stats[:, t, :], xs[:, t, :])),
                         lambda: tiles(lambda t: dve.bn_aggr(mv[:, t, :], stats[:, t, :])),
                         lambda: dve.tensor_scalar(rt[:, 2, :], mv[:, :, 1], EPS, None, ALU.add)]
                steps += rsqrt_steps(dve, rt[:, 2, :], rs[:, :], rt[:, 0, :], rt[:, 1, :])
                steps.append(lambda: tiles(lambda t: dve.tensor_scalar(
                    xn[:, t, :], xs[:, t, :], mv[:, t, 0:1], rs[:, t:t + 1], ALU.subtract, ALU.mult)))
                assert len(steps) == NORM_STEPS
                return steps

            def gate(i, k):
                n = FCH[k][1]
                dve.wait_ge(ge_ev, 3 * i + k + 1)
                if k == 0:
                    wait(dve, y2_mm, i)
                dve.scalar_tensor_tensor(gT[0:n, k, :], OB[1][0:n, :], WF[0:n, F_B1 + k:F_B1 + k + 1],
                                         gel[0:n, k % 2, :], ALU.add, ALU.mult).then_inc(gtd, 1)

            def add_ffn(i):
                dve.wait_ge(y2_mm, i + 1)
                rows = y_cols(i, 0, NTOK)
                dve.tensor_tensor(rows, PJ[1][:, :], rows, ALU.add).then_inc(yd, 1)

            dve.memset(kT[:, :, 0:WIN], 0.0)
            dve.memset(vp[:, :, :, :], 0.0)
            dve.memset(xT[:, 0:1], 0.0)
            dve.memset(next_WF[:, :], 0.0)
            dve.memset(one[:, :], 0.0)
            dve.memset(xs[0:1, 0, DH:P], 0.0)
            dve.memset(gT[:, 2, :], 1.0).then_inc(cleared, 1)
            dve.wait_ge(cleared, 1)

            def slot(i, t):
                if live(i):
                    rotate(i, t, 0)
                    rotate(i, t, 1)
                if live(i, t, 3):
                    row_sums(*lagged(i, t, 3))
                if live(i):
                    rotate(i, t, 2)
                    sum_squares(i, t, 0)
                    rotate(i, t, 3)
                if live(i - 2) and t >= 1:
                    gate(i - 2, t - 1)
                if live(i):
                    sum_squares(i, t, 1)
                side_by_side(i, t)
                if live(i, t, 2):
                    shift(*lagged(i, t, 2))
                if live(i, t, 3):
                    normalize_o(*lagged(i, t, 3))
                if live(i, t, 4):
                    add_attention(*lagged(i, t, 4))
                if live(i - 2) and t == 3:
                    add_ffn(i - 2)

            pipeline(dve, slot)

        @block.gpsimd
        def _(pool):
            def copy_y(i, t):
                g = NT * i + t
                if t == 0:
                    wait(pool, yd, i - NB + 1)
                wait_apart(pool, passed["pool"], xt_mm, g - 1)
                pool.tensor_copy(yc[:, t % 2, :], y_cols(i, t * P, P)).then_inc(ycd, 1)

            def add(i, t, j):
                g = NT * i + t
                pool.wait_ge(rot, 4 * g + j + 1)
                wait(pool, tr_mm, 4 * (g - 2) + j + 1)
                pool.tensor_tensor(qk[:, t % 2, j, :], rotA[:, j % 2, :], rotB[:, j % 2, :], ALU.add).then_inc(added, 1)

            def normalize(i, t, j):
                g = NT * i + t
                pool.wait_ge(newt, RN_STEPS * (g + 1))
                pool.wait_ge(added, 4 * g + j + 1)
                half = qk[:, t % 2, j, :].rearrange("p (h d) -> p h d", d=DH)
                scale = rn[:, t, 8 * j:8 * j + 8].unsqueeze(2).broadcast_to([P, 8, DH])
                pool.tensor_tensor(half, half, scale, ALU.mult).then_inc(normd, 1)

            pool.wait_ge(cleared, 1)
            copy_y(0, 0)

            def layer(l):
                for n in range(TILES):
                    i, t = NB * l + n // NT, n % NT
                    if n < TILES - 1 or not (isinstance(l, int) and l == DEPTH - 1):
                        copy_y(*lagged(i, t, -1))
                    for j in range(4):
                        add(i, t, j)
                    for j in range(4):
                        normalize(i, t, j)
                    if n == 11 and not (isinstance(l, int) and l == DEPTH - 1):
                        pool.wait_ge(wa_ld, 16 * ATTN_DMAS * (l + 1))
                        build_tables(pool, tab, tab_base, W, tabs, (l + 1) % 2)

            layer(0)
            with pool.Fori(1, DEPTH - 1) as l:
                layer(l)
            layer(DEPTH - 1)

        @block.sync
        def _(sp):
            def move_v(i, t):
                g = NT * i + t
                wait_apart(sp, passed["sp"], v_ev, 2 * g + 2)
                wait_apart(sp, passed["sp"], o_mm, g - 1)
                dst, s = vp[:, t % 2], vp_ld[t % 2]
                for e in range(2):
                    at = DH * e
                    for w in range(1, NWIN):
                        sp.dma_start(dst[at:at + 2 * WIN, w, :],
                                     v[WIN * (w - 1):WIN * (w + 1), t % 2, e, :]).then_inc(s, 16)
                    sp.dma_start(dst[at + WIN:at + 2 * WIN, 0, :], v[0:WIN, t % 2, e, :]).then_inc(s, 16)
                    if t > 0:
                        sp.dma_start(dst[at:at + WIN, 0, :], v[P - WIN:P, 1 - t % 2, e, :]).then_inc(s, 16)

            def shift_y(i):
                wait_apart(sp, passed["sp"], resid, NT * i + NT)
                wait_apart(sp, passed["sp"], lnc, NORM_STEPS * i)
                rows = lambda s: y_cols(i, 0, NTOK, s).rearrange("p (t n) -> p t n", n=P)
                sp.dma_start(xs[:, :, 0:DH], rows(slice(0, P))[:, :, 0:DH]).then_inc(xs_ld, 16)
                sp.dma_start(xs[1:P, :, DH:P], rows(slice(0, P - 1))[:, :, DH:P]).then_inc(xs_ld, 16)
                sp.dma_start(xs[0:1, 1:NT, DH:P], rows(slice(P - 1, P))[:, 0:NT - 1, DH:P]).then_inc(xs_ld, 16)

            sp.wait_ge(cleared, 1)
            move_v(0, 0)
            move_v(0, 1)

            def layer(l):
                final = isinstance(l, int) and l == DEPTH - 1
                for n in range(NB):
                    i = NB * l + n
                    if n == 1:
                        wait_apart(sp, passed["sp"], yd, i - 1)
                        if not (isinstance(l, int) and l == 0):
                            wait_apart(sp, passed["sp"], next_ld, 16 * FFN_DMAS * l)
                            sp.dma_start(WF[:, :], next_WF[:, :]).then_inc(wf_ld, 16)
                        if not final:
                            load_attn(sp, a, W, wa_ld, l + 1, (l + 1) % 2 * WSZ)
                    if n == 2 and not final:
                        wait_apart(sp, passed["sp"], wf_ld, 16 * l)
                        load_ffn(sp, a, next_WF, next_ld, l + 1)
                    move_v(i, 2)
                    move_v(i, 3)
                    if not (final and n == NB - 1):
                        move_v(i + 1, 0)
                        move_v(i + 1, 1)
                    shift_y(i)

            layer(0)
            with sp.Fori(1, DEPTH - 1) as l:
                layer(l)
            layer(DEPTH - 1)

    x1 = sb("x1", [P, TILES, P])
    x1_ld, sum_ok, stored = sem("x1_loaded"), sem("summed"), sem("out_stored")
    with nc.Block() as block:
        @block.sync
        def _(sp):
            sp.dma_start(x1[:, :, :], x1_dram[:, :, :]).then_inc(x1_ld, 16)
            sp.wait_ge(sum_ok, 1)
            sp.dma_start(out.rearrange("b (t p) d -> p (b t) d", p=P), x1[:, :, :]).then_inc(stored, 16)
            sp.wait_ge(stored, 16)

        @block.vector
        def _(dve):
            dve.wait_ge(x1_ld, 16)
            dve.tensor_tensor(x1[:, :, :], x1[:, :, :], y[:, :].rearrange("p (t n) -> p t n", n=P),
                              ALU.add).then_inc(sum_ok, 1)


NAMES = ["L0_attn_" + n for n in (
    "x", "ln_g", "ln_b", "Wq", "Wkv", "null_kv", "null_attn_bias", "pb_w0", "pb_b0", "pb_ln0_g", "pb_ln0_b", "pb_w1",
    "pb_b1", "pb_ln1_g", "pb_ln1_b", "pb_w2", "pb_b2", "Wo", "out_ln_g", "out_ln_b")] + ["L0_ffn_" + n for n in (
    "Wqkv", "q_scale", "k_scale", "Wo", "ln_g", "ln_b", "W1", "b1", "W2", "b2")]


def kernel(**inputs):
    import concourse.bacc as _bacc
    from concourse.bass_utils import run_bass_kernel_spmd as _run

    nc = _bacc.Bacc("TRN2", target_bir_lowering=False, num_devices=1)
    arrays, args = {}, {}
    for name in NAMES:
        arr = np.ascontiguousarray(inputs[name])
        arrays[f"in_{name}"] = arr
        args[name] = nc.dram_tensor(f"in_{name}", arr.shape, mybir.dt.from_np(arr.dtype), kind="ExternalInput").ap()
    out = nc.dram_tensor("out_0", (NB, NTOK, P), F32, kind="ExternalOutput").ap()
    build(nc, args, out)
    r = _run(nc, [arrays], core_ids=[0])
    return r.results[0]["out_0"]
```

```python
from contextlib import ExitStack

import numpy as np

import concourse.bass as bass
from concourse import mybir

F32 = mybir.dt.float32
BF16 = mybir.dt.bfloat16
I32 = mybir.dt.int32
ALU = mybir.AluOpType
ACT = mybir.ActivationFunctionType
AX = mybir.AxisListType.X

P = 128
NB, NTOK = 4, 512
NT = NTOK // P
TILES = NB * NT
HEADS, DH = 16, 64
PAIRS = HEADS // 2
INNER = HEADS * DH
DEPTH, WIN = 6, 32
NWIN = P // WIN
FF = int(P * 4 * 2 / 3)
FCH = [(0, 128), (128, 128), (256, FF - 256)]
EPS = 1e-5
NEG = -1e30
BATCHES = DEPTH * NB
RSQRT_MAGIC = float(0x5F375A86)
NEWTON = 3

O_QKV = 0
O_WO = O_QKV + 3 * INNER
O_QS = O_WO + PAIRS * P
WSZ = O_QS + 4 * DH
F_W1 = 0
F_W2 = F_W1 + 2 * FF
F_LNG = F_W2 + 3 * P
F_LNB = F_LNG + 1
F_B1 = F_LNB + 1
FSZ = F_B1 + 6
TSZ = NT * 4 * DH


def rotary_base():
    half = np.arange(0, DH, 2, dtype=np.float32)
    inv_freq = (np.float32(1.0) / np.float32(10000.0) ** (half / np.float32(DH))).astype(np.float32)
    t = np.arange(NTOK, dtype=np.float32)
    freqs = (t[:, None] * inv_freq[None, :]).astype(np.float32)
    base = ((half + np.float32(0.4 * DH)) / np.float32(1.4 * DH)).astype(np.float32)
    power = ((t - NTOK // 2) / np.float32(WIN // 2)).astype(np.float32)
    scale = (base[None, :] ** power[:, None]).astype(np.float32)
    cos, sin = np.cos(freqs), np.sin(freqs)
    both = lambda a, b: np.concatenate([a, b], -1)
    qk = np.float32(8.0)
    inv = np.float32(1.0) / scale
    kinds = [both(cos * scale, cos * scale) * qk, both(-sin * scale, sin * scale) * qk,
             both(cos * inv, cos * inv), both(-sin * inv, sin * inv)]
    table = np.stack(kinds, 1).astype(np.float32)
    return np.ascontiguousarray(table.reshape(NT, P, 4, DH).transpose(1, 0, 2, 3))


def window_masks():
    i = np.arange(P)[:, None] % WIN
    j = np.arange(2 * WIN)[None, :]
    inner = (j >= i) & (j <= i + WIN)
    first = inner & ((np.arange(P)[:, None] >= WIN) | (j >= WIN))
    return np.where(np.stack([inner, first], 1), 0.0, NEG).astype(mybir.dt.np(BF16))


def build(nc, a, out):
    ctx = ExitStack()
    with ctx:
        dram = lambda n, s: nc.dram_tensor(n, s, F32, kind="Internal").ap()
        bias_rows = dram("bias_rows", [HEADS, NTOK + P])

        def keep(name, shape, dt=F32):
            return ctx.enter_context(nc.sbuf_tensor(name, shape, dt))

        banks = [ctx.enter_context(nc.psum_tensor(f"bank{n}", [P, 512], F32)) for n in range(8)]
        ident = keep("ident", [P, P])
        identb = keep("identb", [P, P], BF16)
        masks = keep("masks", [P, 2, 2 * WIN], BF16)
        x = keep("x", [P, TILES, P])
        y = keep("y", [P, TILES * P])
        W = keep("W", [P, 2 * WSZ])
        WF = keep("WF", [P, FSZ])
        tab = keep("tab", [P, 2 * TSZ])
        tab_base = keep("tab_base", [P, NT, 4, DH])
        ins = dict(a)
        with ExitStack() as front:
            stage_a(nc, front, banks, ins, bias_rows, x, ident, identb, masks, y, W, WF, tab, tab_base)
        with ExitStack() as back:
            stage_b(nc, back, banks, ins, out, x, ident, identb, masks, y, W, WF, tab, tab_base)


def wait(eng, sem, value):
    if not isinstance(value, int) or value > 0:
        eng.wait_ge(sem, value)


def wait_apart(eng, passed, sem, value):
    if not isinstance(value, int):
        eng.wait_ge(sem, value).then_inc(passed, 1)
    elif value > 0:
        eng.wait_ge(sem, value)


def layer_of(t, layer):
    return t[layer:layer + 1] if isinstance(layer, int) else t[bass.ds(layer, 1)]


def load_attn(eng, a, W, sem, layer, base):
    def go(o, n, src, split=None):
        dst = W[:, base + o:base + o + n] if isinstance(base, int) else W[:, bass.ds(base + o, n)]
        if split:
            dst = dst.rearrange("p (q n) -> p q n", q=split)
        eng.dma_start(dst, src).then_inc(sem, 16)

    go(O_QKV, 3 * INNER, layer_of(a["L0_ffn_Wqkv"], layer).rearrange("l p n -> (l p) n"))
    go(O_WO, PAIRS * P, layer_of(a["L0_ffn_Wo"], layer).rearrange("l (q p) n -> (l p) q n", p=P), PAIRS)
    h = DH // 2
    for s, name in enumerate(("L0_ffn_q_scale", "L0_ffn_k_scale")):
        src = layer_of(a[name], layer)
        go(O_QS + 2 * s * DH, DH, src.to_broadcast([P, DH]))
        go(O_QS + (2 * s + 1) * DH, h, src[:, h:DH].to_broadcast([P, h]))
        go(O_QS + (2 * s + 1) * DH + h, h, src[:, 0:h].to_broadcast([P, h]))


ATTN_DMAS = 2 + 6


def load_ffn(eng, a, WF, sem, layer):
    def go(o, n, src, rows=P, row0=0):
        eng.dma_start(WF[row0:row0 + rows, o:o + n], src).then_inc(sem, 16)

    go(F_W1, 2 * FF, layer_of(a["L0_ffn_W1"], layer).rearrange("l p n -> (l p) n"))
    for k, (f0, n) in enumerate(FCH):
        go(F_W2 + k * P, P, layer_of(a["L0_ffn_W2"], layer)[:, f0:f0 + n, :].rearrange("l p n -> (l p) n"), n)
    go(F_W2 + 2 * P, P, layer_of(a["L0_ffn_b2"], layer), 1, FCH[2][1])
    go(F_LNG, 1, layer_of(a["L0_ffn_ln_g"], layer).rearrange("l (p o) -> (l p) o", o=1))
    go(F_LNB, 1, layer_of(a["L0_ffn_ln_b"], layer).rearrange("l (p o) -> (l p) o", o=1))
    for s in range(2):
        for k, (f0, n) in enumerate(FCH):
            src = layer_of(a["L0_ffn_b1"], layer)[:, s * FF + f0:s * FF + f0 + n]
            go(F_B1 + 3 * s + k, 1, src.rearrange("l (p o) -> (l p) o", o=1), n)


FFN_DMAS = 1 + 3 + 1 + 2 + 6


def build_tables(pool, tab, tab_base, W, sem, parity):
    def cols(t, o, n):
        return t[:, o:o + n] if isinstance(o, int) else t[:, bass.ds(o, n)]

    dst = cols(tab, parity * TSZ, TSZ).rearrange("p (t k d) -> p t k d", t=NT, k=4)
    qs = cols(W, parity * WSZ + O_QS, 4 * DH).rearrange("p (k d) -> p k d", k=4)
    for t in range(NT):
        last = pool.tensor_tensor(dst[:, t], tab_base[:, t], qs, ALU.mult)
    last.then_inc(sem, 1)


class Chain:

    def __init__(self, eng, sem):
        self.eng, self.sem, self.n = eng, sem, 0

    def __call__(self, ins):
        self.n += 1
        ins.then_inc(self.sem, 1)
        self.eng.wait_ge(self.sem, self.n)


def rsqrt_steps(dve, x, y0, t1, t2):
    steps = [lambda: dve.tensor_scalar(t1.bitcast(I32), x.bitcast(I32), 1, None, ALU.logical_shift_right),
             lambda: dve.tensor_scalar(y0.bitcast(I32), t1.bitcast(I32), -1.0, RSQRT_MAGIC, ALU.mult, ALU.add)]
    for _ in range(NEWTON):
        steps += [lambda: dve.tensor_tensor(t1, y0, y0, ALU.mult),
                  lambda: dve.scalar_tensor_tensor(t2, t1, -0.5, x, ALU.mult, ALU.mult),
                  lambda: dve.scalar_tensor_tensor(y0, t2, 1.5, y0, ALU.add, ALU.mult)]
    return steps


RSQRT_STEPS = 2 + 3 * NEWTON
RN_STEPS = 1 + RSQRT_STEPS
LN_STEPS = 4
NORM_STEPS = 3 + RSQRT_STEPS + 1


def stage_a(nc, ctx, banks, a, bias_rows, x, ident, identb, masks, y, W, WF, tab, tab_base):
    def sb(name, shape, dt=F32):
        return ctx.enter_context(nc.sbuf_tensor(name, shape, dt))

    def sem(name):
        return ctx.enter_context(nc.semaphore(name))

    c_ident = nc.inline_tensor(np.eye(P, dtype=np.float32), "c_ident")
    c_identb = nc.inline_tensor(np.eye(P).astype(mybir.dt.np(BF16)), "c_identb")
    c_masks = nc.inline_tensor(window_masks(), "c_masks")
    c_tab = nc.inline_tensor(rotary_base(), "c_tab")
    c_pos = nc.inline_tensor(np.arange(NTOK).reshape(NT, P).T.astype(np.float32).copy(), "c_pos")
    dr = lambda t: t.ap() if hasattr(t, "ap") else t

    setup_only = ExitStack()

    def once(name, shape, dt=F32):
        return setup_only.enter_context(nc.sbuf_tensor(name, shape, dt))

    xnT = sb("xnT", [P, TILES * P])
    bias = sb("bias", [P, HEADS, NTOK])
    Wq = sb("Wq", [P, INNER])
    Wk2 = sb("Wk2", [P, 2 * DH])
    Wv = sb("Wv", [P, DH])
    WoA = sb("WoA", [P, PAIRS, P])
    nk_sel = sb("nk_sel", [P, PAIRS, HEADS])
    nv_sel = sb("nv_sel", [P, PAIRS, HEADS])
    Wnull = sb("Wnull", [P, HEADS])
    NvWo = sb("NvWo", [HEADS, P])
    nbias = sb("nbias", [P, HEADS])
    lng = sb("lng", [P, 1])
    lnb = sb("lnb", [P, 1])
    og = sb("og", [P, P])
    ob = sb("ob", [P, P])
    stats = sb("stats", [P, TILES, 6])
    mv = sb("mv", [P, TILES, 2])
    rs = sb("rs", [P, TILES])
    rt = sb("rt", [P, 3, TILES])
    nsn = sb("nsn", [P, TILES, HEADS])
    v = sb("v", [P, TILES, DH])
    xn = once("xn", [P, TILES, P])
    WqT = once("WqT", [P, PAIRS, P])
    rows = once("rows", [P, 7, P])
    w1 = once("w1", [P, P])
    w2 = once("w2", [P, HEADS])
    b2c = once("b2c", [HEADS, 1])
    nkv = once("nkv", [P, 2])
    pos = once("pos", [P, NT])
    h = once("h", [P, NT, P])
    h2 = once("h2", [P, NT, P])
    hT = once("hT", [P, NTOK])
    xr = once("xr", [P, TILES * P])
    padded = once("padded", [HEADS, NTOK + P])

    ld = sem("a_loaded")
    ld_w = sem("layer_loaded_first")
    chain = sem("a_dve_chain")
    zero = sem("a_zeroed")
    tr = sem("a_transposed")
    ev = sem("a_evacuated")
    mm = sem("a_product")
    ex = sem("a_exp")
    padded_ok = sem("a_bias_rows_ready")
    h_ok = sem("a_h_affine")
    h_silu = sem("a_h_silu")
    st = sem("a_bias_stored")
    bl = sem("a_bias_loaded")
    tabs = sem("a_tables")
    x_ld, mlp_ld, selected = sem("x_loaded"), sem("mlp_rows_loaded"), sem("a_null_selected")
    n_ld = [0, 0]

    with nc.Block() as block:
        bc = lambda t, n: t.rearrange("(o n) -> o n", o=1).to_broadcast([P, n])
        column = lambda t: t.rearrange("(p o) -> p o", o=1)

        @block.sync
        def _(sp):
            def go(dst, src, on=0):
                n_ld[on] += 1
                sp.dma_start(dst, src).then_inc((ld, mlp_ld)[on], 16)

            for n, name in enumerate(("w0", "b0", "ln0_g", "ln0_b", "b1", "ln1_g", "ln1_b")):
                src = a["L0_attn_pb_" + name]
                go(rows[:, n, :], src.to_broadcast([P, P]) if name == "w0" else bc(src, P), 1)
            go(pos[:, :], dr(c_pos), 1)
            sp.dma_start(x[:, :, :], a["L0_attn_x"].rearrange("b (t p) d -> p (b t) d", p=P)).then_inc(x_ld, 16)
            go(ident[:, :], dr(c_ident))
            go(identb[:, :], dr(c_identb))
            go(masks[:, :, :], dr(c_masks))
            go(tab_base[:, :, :, :], dr(c_tab))
            go(w1[:, :], a["L0_attn_pb_w1"])
            go(w2[:, :], a["L0_attn_pb_w2"])
            go(b2c[:, :], column(a["L0_attn_pb_b2"]))
            go(lng[:, :], column(a["L0_attn_ln_g"]))
            go(lnb[:, :], column(a["L0_attn_ln_b"]))
            go(og[:, :], bc(a["L0_attn_out_ln_g"], P))
            go(ob[:, :], bc(a["L0_attn_out_ln_b"], P))
            go(Wq[:, :], a["L0_attn_Wq"])
            go(Wk2[:, 0:DH], a["L0_attn_Wkv"][:, 0:DH])
            go(Wk2[:, DH:2 * DH], a["L0_attn_Wkv"][:, 0:DH])
            go(Wv[:, :], a["L0_attn_Wkv"][:, DH:2 * DH])
            go(WoA[:, :, :], a["L0_attn_Wo"].rearrange("(q p) n -> p q n", p=P))
            go(nbias[:, :], bc(a["L0_attn_null_attn_bias"], HEADS))
            for which in range(2):
                for e in range(2):
                    src = a["L0_attn_null_kv"][which:which + 1, :].rearrange("o (d c) -> (o d) c", c=1)
                    go(nkv[DH * e:DH * e + DH, which:which + 1], src)
            load_attn(sp, a, W, ld_w, 0, 0)
            load_ffn(sp, a, WF, ld_w, 0)
            sp.wait_ge(padded_ok, 1)
            sp.dma_start(bias_rows, padded[:, :]).then_inc(st, 16)
            sp.wait_ge(st, 16)
            for g in range(4):
                hs = HEADS // 4
                src = bass.AP(tensor=bias_rows.tensor, offset=g * hs * (NTOK + P),
                              ap=[[1, P], [NTOK + P, hs], [1, NTOK]])
                sp.dma_start(bias[:, g * hs:(g + 1) * hs, :], src).then_inc(bl, 16)
            sp.wait_ge(bl, 64)
            sp.wait_ge(ld_w, 16 * (ATTN_DMAS + FFN_DMAS))

        @block.gpsimd
        def _(pool):
            pool.memset(nk_sel[:, :, :], 0.0)
            pool.memset(nv_sel[:, :, :], 0.0).then_inc(zero, 1)
            pool.memset(padded[:, :], NEG).then_inc(zero, 1)
            pool.wait_ge(zero, 2)
            pool.wait_ge(ld, 16 * n_ld[0])
            for which, sel in ((0, nk_sel), (1, nv_sel)):
                for e in range(2):
                    half = slice(DH * e, DH * e + DH)
                    dst = sel[half, :, :].rearrange("p q h -> p (q h)")[:, e::HEADS + 2]
                    pool.tensor_copy(dst, nkv[half, which:which + 1].broadcast_to([DH, PAIRS])).then_inc(selected, 1)
                    pool.wait_ge(selected, 2 * which + e + 1)
            pool.wait_ge(ld_w, 16 * (ATTN_DMAS + FFN_DMAS))
            build_tables(pool, tab, tab_base, W, tabs, 0)
            pool.wait_ge(tabs, 1)

        ALL = 16 * n_ld[0]
        X_BANKS = (6, 2)
        XN_STEPS = 3 * NORM_STEPS + 4

        @block.vector
        def _(dve):
            step = Chain(dve, chain)

            def norm(dst, src, n, eps=EPS):
                for t in range(n):
                    last = dve.bn_stats(stats[:, t, :], src(t))
                step(last)
                for t in range(n):
                    last = dve.bn_aggr(mv[:, t, :], stats[:, t, :])
                step(last)
                step(dve.tensor_scalar(rt[:, 2, 0:n], mv[:, 0:n, 1], eps, None, ALU.add))
                for s in rsqrt_steps(dve, rt[:, 2, 0:n], rs[:, 0:n], rt[:, 0, 0:n], rt[:, 1, 0:n]):
                    step(s())
                for t in range(n):
                    last = dve.tensor_scalar(dst(t), src(t), mv[:, t, 0:1], rs[:, t:t + 1], ALU.subtract, ALU.mult)
                step(last)

            def affine(dst, g, b):
                row = lambda r: r.unsqueeze(1).broadcast_to([P, NT, P])
                step(dve.tensor_tensor(dst, dst, row(g), ALU.mult))
                dve.tensor_tensor(dst, dst, row(b), ALU.add).then_inc(h_ok, 1)

            dve.wait_ge(mlp_ld, 16 * n_ld[1])
            for t in range(NT):
                last = dve.scalar_tensor_tensor(h[:, t, :], rows[:, 0, :], pos[:, t:t + 1], rows[:, 1, :],
                                                ALU.mult, ALU.add)
            step(last)
            for layer in range(2):
                if layer:
                    dve.wait_ge(mm, 1)
                    row = rows[:, 4, :].unsqueeze(1).broadcast_to([P, NT, P])
                    step(dve.tensor_tensor(h[:, :, :], banks[1][:, :].rearrange("p (t n) -> p t n", t=NT), row, ALU.add))
                norm(lambda t: h[:, t, :], lambda t: h[:, t, :], NT)
                affine(h[:, :, :], rows[:, 2 + 3 * layer, :], rows[:, 3 + 3 * layer, :])
                if layer == 0:
                    dve.wait_ge(x_ld, 16)
                    norm(lambda t: xn[:, t, :], lambda t: x[:, t, :], TILES)
                dve.wait_ge(ex, 1 + layer)
                step(dve.tensor_scalar(h2[:, :, :], h2[:, :, :], 1.0, None, ALU.add))
                step(dve.reciprocal(h2[:, :, :], h2[:, :, :]))
                dve.tensor_tensor(h[:, :, :], h[:, :, :], h2[:, :, :], ALU.mult).then_inc(h_silu, 1)
                if layer == 0:
                    norm(lambda t: xn[:, t, :], lambda t: xn[:, t, :], TILES)
                    assert step.n == XN_STEPS
            dve.wait_ge(ld, ALL)
            dve.wait_ge(mm, 4)
            dve.wait_ge(zero, 2)
            dve.tensor_scalar(padded[:, P - 1:P - 1 + NTOK], banks[3][0:HEADS, :], b2c[:, 0:1], None,
                              ALU.add).then_inc(padded_ok, 1)
            step(dve.tensor_copy(NvWo[:, :], banks[5][0:HEADS, 0:P]))
            nb = nbias[:, :].unsqueeze(1).broadcast_to([P, TILES, HEADS])
            dve.wait_ge(mm, 5)
            src = banks[6][:, 0:TILES * HEADS].rearrange("p (t n) -> p t n", t=TILES)
            step(dve.tensor_scalar(nsn[:, :, :], src, -float(DH) ** -0.5, None, ALU.mult))
            step(dve.tensor_tensor(nsn[:, :, :], nsn[:, :, :], nb, ALU.subtract))

        @block.scalar
        def _(act):
            act.wait_ge(ld, ALL)
            for g, bank in ((0, 2), (1, 4)):
                act.wait_ge(tr, 1 + g)
                act.activation(WqT[:, 4 * g:4 * g + 4, :], banks[bank][:, :].rearrange("p (q n) -> p q n", q=4),
                               ACT.Copy).then_inc(ev, 1)

            def silu_part(layer, turned):
                act.wait_ge(h_ok, 1 + layer)
                act.activation(h2[:, :, :], h[:, :, :], ACT.Exp, scale=-1.0).then_inc(ex, 1)
                act.wait_ge(tr, turned)
                act.activation(hT[:, :], banks[0][:, :], ACT.Copy).then_inc(ev, 1)

            silu_part(0, 3)
            act.wait_ge(mm, 2)
            act.activation(Wnull[:, :], banks[7][:, 0:HEADS], ACT.Copy).then_inc(ev, 1)
            for b in range(NB):
                act.wait_ge(tr, b + 4)
                act.activation(xr[:, b * NTOK:(b + 1) * NTOK], banks[X_BANKS[b % 2]][:, ::-1], ACT.Identity,
                               bias=lnb[:, 0:1], scale=lng[:, 0:1])
                act.activation(xnT[:, b * NTOK:(b + 1) * NTOK], banks[X_BANKS[b % 2]][:, :], ACT.Identity,
                               bias=lnb[:, 0:1], scale=lng[:, 0:1]).then_inc(ev, 1)
            silu_part(1, 8)
            for g in range(2):
                act.wait_ge(mm, 6 + g)
                act.activation(v[:, 8 * g:8 * g + 8, :], banks[g][:, :].rearrange("p (t n) -> p t n", t=8),
                               ACT.Copy).then_inc(ev, 1)

        @block.tensor
        def _(pe):
            pe.wait_ge(ld, ALL)
            for g, bank in ((0, 2), (1, 4)):
                for q in range(4):
                    w = Wq[:, (4 * g + q) * P:(4 * g + q + 1) * P]
                    last = pe.transpose(banks[bank][:, q * P:(q + 1) * P], w, ident[:, :])
                last.then_inc(tr, 1)

            def turn_h(layer):
                pe.wait_ge(h_silu, 1 + layer)
                for t in range(NT):
                    last = pe.transpose(banks[0][:, t * P:(t + 1) * P], h[:, t, :], ident[:, :])
                last.then_inc(tr, 1)

            turn_h(0)
            pe.wait_ge(ev, 3)
            for t in range(NT):
                last = pe.matmul(banks[1][:, t * P:(t + 1) * P], hT[:, t * P:(t + 1) * P], w1[:, :],
                                 start=True, stop=True)
            last.then_inc(mm, 1)
            pe.wait_ge(selected, 4)
            for q in range(PAIRS):
                last = pe.matmul(banks[7][:, 0:HEADS], WqT[:, q, :], nk_sel[:, q, :], start=q == 0, stop=q == PAIRS - 1)
            last.then_inc(mm, 1)
            for q in range(PAIRS):
                last = pe.matmul(banks[5][0:HEADS, 0:P], nv_sel[:, q, :], WoA[:, q, :],
                                 start=q == 0, stop=q == PAIRS - 1)
            last.then_inc(mm, 1)
            pe.wait_ge(chain, XN_STEPS)
            for b in range(NB):
                if b >= 2:
                    pe.wait_ge(ev, 3 + b)
                for t in range(NT):
                    last = pe.transpose(banks[X_BANKS[b % 2]][:, t * P:(t + 1) * P], xn[:, NT * b + t, :], ident[:, :])
                last.then_inc(tr, 1)
            turn_h(1)
            pe.wait_ge(ev, 9)
            last = pe.matmul(banks[3][0:HEADS, :], w2[:, :], hT[:, :], start=True, stop=True)
            last.then_inc(mm, 1)
            for t in range(TILES):
                last = pe.matmul(banks[6][:, t * HEADS:(t + 1) * HEADS], xnT[:, t * P:(t + 1) * P], Wnull[:, :],
                                 start=True, stop=True)
            last.then_inc(mm, 1)
            for g in range(2):
                for t in range(8):
                    last = pe.matmul(banks[g][:, t * DH:(t + 1) * DH], xr[:, (8 * g + t) * P:(8 * g + t + 1) * P],
                                     Wv[:, :], start=True, stop=True)
                last.then_inc(mm, 1)

    setup_only.close()
    qT = sb("qT_a", [P, 2, NTOK])
    kT = sb("kT_a", [P, NTOK])
    vb = sb("vb", [P, NT, DH])
    nsb = sb("nsb", [P, NT, HEADS])
    pr = sb("pr", [P, 2, 1280])
    pT = sb("pT", [P, 4, 1280])
    oT = sb("oT_a", [P, PAIRS, NTOK])
    att = sb("att", [P, NT, P])
    summed = sb("summed", [P, NT, P])
    pn = sb("pn", [P, NT, HEADS])
    pnT = sb("pnT", [HEADS, NTOK])
    negm = sb("negm", [P, 2, NT])
    rsum = sb("rsum", [P, 2, NT])
    rinv = sb("rinv", [P, 2, NT])
    pex = sb("pex", [P, 2, NT])

    q_mm, k_mm, s_mm, t_mm, o_mm, w_mm, pn_mm = (sem("a_" + n) for n in (
        "q_filled", "k_filled", "scores_filled", "pT_filled", "o_filled", "wo_filled", "pnT_filled"))
    q_ev, k_ev, v_ev, t_ev_act, t_ev_dve, o_ev, pn_ev = (sem("a_" + n) for n in (
        "q_copied", "k_copied", "v_copied", "pT_copied_act", "pT_copied_dve", "o_copied", "pnT_copied"))
    s_sub, p_exp, n_exp, p_norm, small, tail, w_read, shifted = (sem("a_" + n) for n in (
        "scores_biased", "p_exp", "null_exp", "p_normed", "row_sums", "tail", "wo_read", "null_shifted"))
    passed = {e: sem("a_" + e + "_passed_wait") for e in ("dve", "pool")}
    KLEN = [P * (t + 1) for t in range(NT)]
    PR_AT = [0, 128, 384, 768]
    TAIL_STEPS = 2 * NORM_STEPS + 4
    PT_AT = [0, 512, 896, 1152]
    PT_BANKS = [(0,), (1,), (2, 3)]
    T_BANKS, O_BANK, Q_BANK, WO_BANK = banks[3:6], banks[6], banks[7], banks[2]
    SCORES = [banks[0][:, 0:P], banks[0][:, P:3 * P], banks[1][:, 0:3 * P], banks[2][:, :]]

    with nc.Block() as block:
        @block.gpsimd
        def _(pool):
            with pool.Fori(0, NB) as b:
                pool.wait_ge(o_mm, b * PAIRS)
                wait_apart(pool, passed["pool"], shifted, b * HEADS)
                pool.tensor_copy(nsb[:, :, :], nsn[:, bass.ds(b * NT, NT), :])
                pool.tensor_copy(vb[:, :, :], v[:, bass.ds(b * NT, NT), :]).then_inc(v_ev, 1)

        @block.tensor
        def _(pe):
            with pe.Fori(0, NB) as b:
                def q_proj(q):
                    pe.wait_ge(q_ev, b * PAIRS + q)
                    pe.matmul(Q_BANK[:, :], Wq[:, q * P:(q + 1) * P], xnT[:, bass.ds(b * NTOK, NTOK)],
                              start=True, stop=True).then_inc(q_mm, 1)

                def scores(n):
                    q, e = divmod(n, 2)
                    rows_ = slice(DH * e, DH * e + DH)
                    pe.wait_ge(q_ev, b * PAIRS + q + 1)
                    for t in range(NT):
                        if t == 3 and n == 0:
                            pe.wait_ge(w_read, b)
                        if n and t != 1:
                            pe.wait_ge(s_sub, b * HEADS * NT + (n - 1) * NT + max(t + 1, 2))
                        pe.matmul(SCORES[t], qT[rows_, q % 2, t * P:(t + 1) * P],
                                  kT[rows_, NTOK - KLEN[t]:NTOK], start=True, stop=True).then_inc(s_mm, 1)

                def turn(n):
                    pe.wait_ge(p_norm, (b * HEADS + n + 1))
                    for g, group in enumerate(PT_BANKS):
                        if g == 0:
                            pe.wait_ge(t_ev_act, b * HEADS + n)
                        else:
                            pe.wait_ge(t_ev_dve, b * 2 * HEADS + max(0, 2 * (n - 1) + g))
                        col = 0
                        for j in group:
                            for t in range(j, NT):
                                at = PR_AT[t] + (t - j) * P
                                last = pe.transpose(T_BANKS[g][:, col:col + P], pr[:, n % 2, at:at + P], ident[:, :])
                                col += P
                        last.then_inc(t_mm, 1)

                def product(q):
                    if q == 0:
                        pe.wait_ge(pn_ev, b)
                        pe.wait_ge(v_ev, b + 1)
                    else:
                        pe.wait_ge(o_ev, b * PAIRS + q)
                    pe.wait_ge(t_ev_act, b * HEADS + 2 * q + 2)
                    pe.wait_ge(t_ev_dve, b * 2 * HEADS + 4 * q + 4)
                    for j in range(NT):
                        for e in range(2):
                            last = pe.matmul(O_BANK[DH * e:DH * e + DH, j * P:NTOK], vb[:, NT - 1 - j, :],
                                             pT[:, (2 * q + e) % 4, PT_AT[j]:PT_AT[j] + NTOK - j * P],
                                             start=j == 0, stop=j == NT - 1)
                    last.then_inc(o_mm, 1)

                pe.wait_ge(s_sub, b * HEADS * NT)
                pe.matmul(banks[0][:, :], Wk2[:, :], xnT[:, bass.ds(b * NTOK, NTOK)],
                          start=True, stop=True).then_inc(k_mm, 1)
                q_proj(0)
                pe.wait_ge(k_ev, b + 1)
                for n in range(HEADS + 2):
                    if n < HEADS:
                        scores(n)
                    if n % 2 == 0 and n // 2 + 1 < PAIRS:
                        q_proj(n // 2 + 1)
                    if n >= 3 and n % 2:
                        product((n - 3) // 2)
                    if 1 <= n <= HEADS:
                        turn(n - 1)
                pe.wait_ge(o_ev, b * PAIRS + PAIRS)
                for t in range(NT):
                    last = pe.transpose(O_BANK[0:HEADS, t * P:(t + 1) * P], pn[:, t, :], ident[:, :])
                last.then_inc(pn_mm, 1)
                pe.wait_ge(pn_ev, b + 1)
                for t in range(NT):
                    for q in range(PAIRS):
                        pe.matmul(WO_BANK[:, t * P:(t + 1) * P], oT[:, q, t * P:(t + 1) * P], WoA[:, q, :],
                                  start=q == 0, stop=False)
                    last = pe.matmul(WO_BANK[:, t * P:(t + 1) * P], pnT[:, t * P:(t + 1) * P], NvWo[:, :],
                                     start=False, stop=True)
                last.then_inc(w_mm, 1)

        @block.scalar
        def _(act):
            with act.Fori(0, NB) as b:
                def q_copy(q):
                    act.wait_ge(q_mm, b * PAIRS + q + 1)
                    if q >= 2:
                        act.wait_ge(s_mm, b * HEADS * NT + 2 * (q - 1) * NT)
                    act.activation(qT[:, q % 2, :], Q_BANK[:, :], ACT.Copy,
                                   scale=float(DH) ** -0.5).then_inc(q_ev, 1)

                act.wait_ge(k_mm, b + 1)
                act.activation(kT[:, :], banks[0][:, ::-1], ACT.Copy).then_inc(k_ev, 1)
                q_copy(0)
                for n in range(HEADS + 2):
                    if n < HEADS:
                        for t in range(NT):
                            act.wait_ge(s_sub, b * HEADS * NT + n * NT + t + 1)
                            row = pr[:, n % 2, PR_AT[t]:PR_AT[t] + KLEN[t]]
                            last = act.activation(row, row, ACT.Exp, scale=-1.0, bias=negm[:, n % 2, t:t + 1],
                                                  accum_out=rsum[:, n % 2, t:t + 1])
                        last.then_inc(p_exp, 1)
                        act.wait_ge(shifted, b * HEADS + n + 1)
                        act.activation(pex[:, n % 2, :], pex[:, n % 2, :], ACT.Exp).then_inc(n_exp, 1)
                    if n % 2 == 0 and n // 2 + 1 < PAIRS:
                        q_copy(n // 2 + 1)
                    if 1 <= n <= HEADS:
                        m = n - 1
                        act.wait_ge(t_mm, b * 3 * HEADS + 3 * m + 1)
                        if m >= 4:
                            act.wait_ge(o_mm, b * PAIRS + m // 2 - 1)
                        act.activation(pT[:, m % 4, 0:512], T_BANKS[0][:, :], ACT.Copy).then_inc(t_ev_act, 1)
                    if n >= 3 and n % 2 == 1:
                        q = (n - 3) // 2
                        act.wait_ge(o_mm, b * PAIRS + q + 1)
                        act.activation(oT[:, q, :], O_BANK[:, :], ACT.Copy).then_inc(o_ev, 1)
                act.wait_ge(pn_mm, b + 1)
                act.activation(pnT[:, :], O_BANK[0:HEADS, :], ACT.Copy).then_inc(pn_ev, 1)

        @block.vector
        def _(dve):
            def finish(b):
                k = [0]

                def step(ins):
                    k[0] += 1
                    ins.then_inc(tail, 1)
                    wait_apart(dve, passed["dve"], tail, TAIL_STEPS * b + k[0])

                def tiles(make):
                    for t in range(NT):
                        last = make(t)
                    step(last)

                def norm(dst, src):
                    tiles(lambda t: dve.bn_stats(stats[:, t, :], src[:, t, :]))
                    tiles(lambda t: dve.bn_aggr(mv[:, t, :], stats[:, t, :]))
                    step(dve.tensor_scalar(rt[:, 2, 0:NT], mv[:, 0:NT, 1], EPS, None, ALU.add))
                    for s in rsqrt_steps(dve, rt[:, 2, 0:NT], rs[:, 0:NT], rt[:, 0, 0:NT], rt[:, 1, 0:NT]):
                        step(s())
                    tiles(lambda t: dve.tensor_scalar(dst(t), src[:, t, :], mv[:, t, 0:1], rs[:, t:t + 1],
                                                      ALU.subtract, ALU.mult))

                of = lambda n: slice(b * n, b * n + n) if isinstance(b, int) else bass.ds(b * n, n)
                row = lambda r: r[:, :].unsqueeze(1).broadcast_to([P, NT, P])
                xb, yb = x[:, of(NT), :], y[:, of(NTOK)]
                norm(lambda t: att[:, t, :], att)
                step(dve.tensor_tensor(att[:, :, :], att[:, :, :], row(og), ALU.mult))
                step(dve.tensor_tensor(att[:, :, :], att[:, :, :], row(ob), ALU.add))
                step(dve.tensor_tensor(summed[:, :, :], att[:, :, :], xb, ALU.add))
                step(dve.tensor_tensor(xb, att[:, :, :], xb, ALU.add))
                norm(lambda t: yb[:, t * P:(t + 1) * P], summed)
                assert k[0] == TAIL_STEPS

            def sequence(b):
                def biased(n):
                    for t in range(NT):
                        if t == 0:
                            wait(dve, t_mm, b * 3 * HEADS + max(0, 3 * (n - 1)))
                        if t != 1:
                            wait_apart(dve, passed["dve"], s_mm, b * HEADS * NT + n * NT + max(t + 1, 2))
                        at = PR_AT[t]
                        dve.tensor_tensor_reduce(pr[:, n % 2, at:at + KLEN[t]], SCORES[t], bias[:, n, 0:KLEN[t]], -1.0,
                                                 nsb[:, t, n:n + 1], ALU.add, ALU.min,
                                                 negm[:, n % 2, t:t + 1]).then_inc(s_sub, 1)

                def null_shift(n):
                    i = n % 2
                    wait(dve, s_sub, (b * HEADS + n + 1) * NT)
                    dve.tensor_tensor(pex[:, i, :], negm[:, i, :], nsb[:, :, n], ALU.subtract).then_inc(shifted, 1)

                def sums(n):
                    i = n % 2
                    k = 3 * (b * HEADS + n)
                    wait(dve, n_exp, b * HEADS + n + 1)
                    wait(dve, p_exp, b * HEADS + n + 1)
                    dve.tensor_tensor(rsum[:, i, :], rsum[:, i, :], pex[:, i, :], ALU.add).then_inc(small, 1)
                    wait(dve, small, k + 1)
                    dve.reciprocal(rinv[:, i, :], rsum[:, i, :]).then_inc(small, 1)
                    wait(dve, small, k + 2)
                    dve.tensor_tensor(pn[:, :, n], pex[:, i, :], rinv[:, i, :], ALU.mult).then_inc(small, 1)
                    for t in range(NT):
                        row = pr[:, i, PR_AT[t]:PR_AT[t] + KLEN[t]]
                        last = dve.tensor_scalar(row, row, rinv[:, i, t:t + 1], None, ALU.mult)
                    last.then_inc(p_norm, 1)

                wait(dve, v_ev, b + 1)
                wait(dve, pn_mm, b)
                for n in range(HEADS + 2):
                    if 1 <= n <= HEADS:
                        sums(n - 1)
                    if n < HEADS:
                        biased(n)
                        null_shift(n)
                    if 1 <= n <= HEADS:
                        m = n - 1
                        if m >= 4:
                            wait(dve, o_mm, b * PAIRS + m // 2 - 1)
                        for g, at in ((1, 512), (2, 896)):
                            wait(dve, t_mm, b * 3 * HEADS + 3 * m + g + 1)
                            dve.tensor_copy(pT[:, m % 4, at:at + 384],
                                            T_BANKS[g][:, 0:384]).then_inc(t_ev_dve, 1)
                if not (isinstance(b, int) and b == 0):
                    finish(b - 1)
                wait(dve, w_mm, b + 1)
                dve.tensor_copy(att[:, :, :], WO_BANK[:, :].rearrange("p (t n) -> p t n", t=NT)).then_inc(w_read, 1)
                wait(dve, w_read, b + 1)

            sequence(0)
            with dve.Fori(1, NB) as b:
                sequence(b)
            finish(NB - 1)


def stage_b(nc, ctx, banks, a, out, x, ident, identb, masks, y, W, WF, tab, tab_base):
    def sb(name, shape, dt=F32):
        return ctx.enter_context(nc.sbuf_tensor("b_" + name, shape, dt))

    def sem(name):
        return ctx.enter_context(nc.semaphore("b_" + name))

    yc = sb("yc", [P, 2, P])
    xT = sb("xT", [P, NTOK + 1])
    sq = sb("sq", [P, 4, 512])
    rotA = sb("rotA", [P, 2, 512])
    rotB = sb("rotB", [P, 2, 512])
    qk = sb("qk", [P, 2, 4, 512])
    ssq = sb("ssq", [P, 2, 2 * HEADS + NT])
    rn = sb("rn", [P, NT, 2 * HEADS + NT])
    nt = sb("nt", [P, 2, 2 * HEADS + NT])
    qT = sb("qT", [P, 2, PAIRS, P])
    kT = sb("kT", [P, PAIRS, WIN + NTOK])
    v = sb("v", [P, 2, 2, 512])
    vp = sb("vp", [P, 2, NWIN, 512])
    pr = sb("pr", [P, 2, PAIRS, 2, 2 * WIN])
    pT = sb("pT", [P, PAIRS, P])
    o = sb("o", [P, PAIRS, 2, DH])
    oT = sb("oT", [P, PAIRS, P])
    mx = sb("mx", [P, 2, PAIRS])
    rsum = sb("rsum", [P, 2, PAIRS])
    rinv = sb("rinv", [P, 2, PAIRS])
    xs = sb("xs", [P, NT, P])
    xn = sb("xn", [P, NT, P])
    hT = sb("hT", [P, NTOK])
    gel = sb("gel", [P, 2, 512])
    next_WF = sb("next_WF", [P, FSZ])
    gT = sb("gT", [P, 3, 512])
    stats = sb("stats", [P, NT, 6])
    mv = sb("mv", [P, NT, 2])
    nmean = sb("nmean", [P, NT])
    one = sb("one", [1, 3])

    qk_mm, v_mm, tr_mm, s_mm, pt_mm, o_mm, ot_mm, wo_mm, xn_mm, ga_mm, y2_mm, xt_mm = (
        sem(n + "_filled") for n in ("qk", "v", "qkT", "scores", "pT", "o", "oT", "wo", "xnT", "ffn", "y2", "xT"))
    sq_ev, tr_ev, v_ev, p_exp, pt_ev, ot_ev, xnd, xn_ev, ge_ev, xt_ev = (
        sem(n) for n in ("squared", "qkT_copied", "v_copied", "p_exp", "pT_copied", "oT_copied", "y_normed",
                         "hT_copied", "gelu", "xT_copied"))
    tables_in = sem("function_table_loaded")
    rot, ssqd, newt, mxd, subd, sumd, invd, onorm, resid, lnc, gtd, yd = (
        sem(n) for n in ("rot_products", "sums_of_squares", "rsqrt_steps", "row_max", "scores_shifted",
                         "row_sums", "inverse_sums", "o_normed", "attn_added", "ln_steps", "gated", "ffn_added"))
    cleared, added, normd, ycd, tabs = (
        sem(n) for n in ("cleared", "rot_added", "qk_normed", "y_copied", "tables"))
    vp_ld = [sem("vp_loaded_even"), sem("vp_loaded_odd")]
    xs_ld, wa_ld, wf_ld, next_ld = (sem(n) for n in ("xs_loaded", "attn_weights", "ffn_weights", "next_ffn_weights"))
    passed = {e: sem(e + "_passed_wait") for e in ("pe", "dve", "pool", "sp")}
    PJ, TR, SC, OB = banks[0:2], banks[2:4], banks[4:6], banks[6:8]

    def lagged(i, t, lag):
        return i + (t - lag) // NT, (t - lag) % NT

    def live(i, t=0, lag=0):
        i = lagged(i, t, lag)[0]
        return not isinstance(i, int) or 0 <= i < BATCHES

    def cols(tensor, i, size, off, n):
        if isinstance(i, int):
            base = (i // NB) % 2 * size + off
            return tensor[:, base:base + n]
        return tensor[:, bass.ds((i // NB) % 2 * size + off, n)]

    def y_cols(i, off, n, rows=slice(0, P)):
        if isinstance(i, int):
            base = (i % NB) * NTOK + off
            return y[rows, base:base + n]
        return y[rows, bass.ds((i % NB) * NTOK + off, n)]

    def vp_count(i, t):
        return 16 * (18 * i + (8 if t == 0 else 18)) if t % 2 == 0 else 16 * (20 * i + (10 if t == 1 else 20))

    def attn_ready(i):
        return 16 * ATTN_DMAS * (i // NB)

    def pipeline(eng, slot):
        for i in range(2):
            for t in range(NT):
                slot(i, t)
        with eng.Fori(2, BATCHES - 1) as i:
            for t in range(NT):
                slot(i, t)
        for i in range(BATCHES - 1, BATCHES + 2):
            for t in range(NT):
                slot(i, t)

    with nc.Block() as block:
        @block.tensor
        def _(pe):
            pe.wait_ge(cleared, 2)

            def turn_x(i, t):
                g = NT * i + t
                wait(pe, ycd, g + 1)
                pe.transpose(PJ[1][:, 0:P], yc[:, t % 2, :], ident[:, :]).then_inc(xt_mm, 1)

            def project(i, t, j):
                g = NT * i + t
                if j == 0:
                    wait(pe, xt_ev, g + 1)
                    if t == 0:
                        wait(pe, wa_ld, attn_ready(i))
                    if isinstance(i, int):
                        wait(pe, rot, 4 * g - 1)
                        wait(pe, v_ev, 2 * (g - 3) + 1)
                    wait(pe, resid, g - 4)
                if j == 1:
                    if t == 1 and live(i - 2):
                        wait(pe, xn_ev, i - 1)
                    if t == 0 and live(i - 3):
                        wait(pe, yd, i - 2)
                if j >= 2:
                    pe.wait_ge(rot, 4 * g + j - 1)
                pe.matmul(PJ[j % 2][:, :], xT[:, t * P:(t + 1) * P], cols(W, i, WSZ, O_QKV + 512 * j, 512),
                          start=True, stop=True).then_inc(qk_mm, 1)

            def turn_qk(i, t, j):
                g = NT * i + t
                pe.wait_ge(normd, 4 * g + j + 1)
                if j < 2:
                    if isinstance(i, int):
                        wait(pe, tr_ev, 4 * g + j - 1)
                        wait(pe, pt_ev, 2 * (g - 3) + j + 1)
                    wait(pe, ot_ev, 2 * (g - 4) + j + 1)
                else:
                    pe.wait_ge(tr_ev, 4 * g + j - 1)
                for q in range(4):
                    last = pe.transpose(TR[j % 2][:, q * P:(q + 1) * P], qk[:, t % 2, j, q * P:(q + 1) * P],
                                        ident[:, :])
                last.then_inc(tr_mm, 1)

            def turn_p(i, t, j, fed):
                g = NT * i + t
                wait(pe, p_exp, 2 * g + 2)
                if fed:
                    wait(pe, tr_ev, 4 * (g + 2) + j + 3)
                else:
                    wait(pe, ot_ev, 2 * (g - 2) + j + 1)
                for q in range(4):
                    last = pe.transpose(TR[j][:, q * P:(q + 1) * P],
                                        pr[:, t % 2, 4 * j + q, :, :].rearrange("p e k -> p (e k)"), ident[:, :])
                last.then_inc(pt_mm, 1)

            def turn_o(i, t, j, fed):
                g = NT * i + t
                wait(pe, onorm, 2 * g + 2)
                if fed:
                    wait(pe, pt_ev, 2 * (g + 1) + j + 1)
                else:
                    wait(pe, ot_ev, 2 * (g - 1) + j + 1)
                for q in range(4):
                    last = pe.transpose(TR[j][:, q * P:(q + 1) * P],
                                        o[:, 4 * j + q, :, :].rearrange("p e d -> p (e d)"), ident[:, :])
                last.then_inc(ot_mm, 1)

            def project_v(i, t, j, fed, before):
                g = NT * i + t
                if fed:
                    wait(pe, rot, 4 * (g + 2) + j + 3)
                else:
                    wait(pe, v_ev, 2 * (g - 1) + j + 1)
                    for s, value in before:
                        wait(pe, s, value)
                w = cols(W, i, WSZ, O_QKV + 2 * INNER, INNER).rearrange("p (q e d) -> p e q d", e=2, d=DH)
                pe.matmul(PJ[j][:, :].rearrange("p (q d) -> p q d", d=DH), xT[:, t * P:(t + 1) * P], w[:, j],
                          start=True, stop=True).then_inc(v_mm, 1)

            def mask_scores(i, t):
                g = NT * i + t
                pe.wait_ge(tr_ev, 4 * g + 4)
                wait(pe, subd, 2 * g)
                m = masks[:, 1 if t == 0 else 0, :].unsqueeze(1).broadcast_to([P, PAIRS, 2 * WIN])
                for e in range(2):
                    pe.matmul(SC[e][:, :].rearrange("p (q k) -> p q k", q=PAIRS), identb[:, :], m,
                              start=True, stop=False, skip_group_check=True)

            def scores(i, t, w):
                rows = slice(WIN * w, WIN * w + WIN)
                at = t * P + w * WIN
                for q in range(PAIRS):
                    for e in range(2):
                        half = slice(DH * e, DH * e + DH)
                        last = pe.matmul(SC[e][rows, q * 2 * WIN:(q + 1) * 2 * WIN], qT[half, t % 2, q, rows],
                                         kT[half, q, at:at + 2 * WIN], start=False, stop=True,
                                         skip_group_check=True)
                if w == NWIN - 1:
                    last.then_inc(s_mm, 1)

            def product(i, t, windows):
                g = NT * i + t
                if windows[0] == 0:
                    pe.wait_ge(pt_ev, 2 * g + 2)
                    wait_apart(pe, passed["pe"], vp_ld[t % 2], vp_count(i, t))
                for w in windows:
                    rows = slice(WIN * w, WIN * w + WIN)
                    for q in range(PAIRS):
                        for e in range(2):
                            half = slice(DH * e, DH * e + DH)
                            last = pe.matmul(OB[e][rows, q * DH:(q + 1) * DH], pT[half, q, rows],
                                             vp[half, t % 2, w, q * DH:(q + 1) * DH], start=True, stop=True)
                if windows[-1] == NWIN - 1:
                    last.then_inc(o_mm, 1)

            def project_o(i, t, pairs):
                g = NT * i + t
                if pairs[0] == 0:
                    pe.wait_ge(ot_ev, 2 * g + 2)
                w = cols(W, i, WSZ, O_WO, PAIRS * P)
                for q in pairs:
                    last = pe.matmul(PJ[0][:, 0:P], oT[:, q, :], w[:, q * P:(q + 1) * P],
                                     start=q == 0, stop=q == PAIRS - 1)
                if pairs[-1] == PAIRS - 1:
                    last.then_inc(wo_mm, 1)

            def turn_xn(i):
                pe.wait_ge(xnd, i + 1)
                for t in range(NT):
                    last = pe.transpose(PJ[1][:, t * P:(t + 1) * P], xn[:, t, :], ident[:, :])
                last.then_inc(xn_mm, 1)

            def expand(i, k):
                n = FCH[k][1]
                pe.wait_ge(xn_ev, i + 1)
                if k == 0:
                    wait(pe, wf_ld, 16 * (i // NB))
                for s, bank in ((1, OB[0]), (0, OB[1])):
                    c = F_W1 + s * FF + FCH[k][0]
                    last = pe.matmul(bank[0:n, :], WF[:, c:c + n], hT[:, :], start=True, stop=True)
                last.then_inc(ga_mm, 1)

            def contract(i):
                pe.wait_ge(gtd, 3 * i + 3)
                for t in range(NT):
                    for k, (_, n) in enumerate(FCH):
                        n += k == 2
                        last = pe.matmul(PJ[1][:, t * P:(t + 1) * P], gT[0:n, k, t * P:(t + 1) * P],
                                         WF[0:n, F_W2 + k * P:F_W2 + (k + 1) * P], start=k == 0, stop=k == 2)
                last.then_inc(y2_mm, 1)

            turn_x(0, 0)

            def slot(i, t):
                g = NT * i + t
                fed = live(i)
                ffn = live(i - 2)
                for j in range(4):
                    if live(i, t, 2) and j < 2:
                        if j == 0:
                            mask_scores(*lagged(i, t, 2))
                        scores(*lagged(i, t, 2), 2 * j)
                        scores(*lagged(i, t, 2), 2 * j + 1)
                    if fed:
                        project(i, t, j)
                    if ffn and t == 1 and j == 0:
                        if fed:
                            pe.wait_ge(xt_ev, g + 1)
                        elif live(i, t, 3):
                            pe.wait_ge(v_ev, 2 * (g - 3) + 2)
                        else:
                            pe.wait_ge(yd, i - 2)
                        turn_xn(i - 2)
                    if live(i, t, 1):
                        turn_qk(*lagged(i, t, 1), j)
                    if j == 1 and ffn and t >= 1:
                        if live(i, t, 4):
                            wait(pe, onorm, 2 * (g - 4) + 2)
                        wait(pe, gtd, 3 * (i - 2) + t - 1)
                        expand(i - 2, t - 1)
                before = [(resid, g - 4)], [(xn_ev, i - 1)] if t == 1 else [(yd, i - 2)] if t == 0 else []
                for j in range(2):
                    if live(i, t, 3):
                        turn_p(*lagged(i, t, 3), j, live(i, t, 1))
                    if j == 1 and live(i, t, 4):
                        turn_o(*lagged(i, t, 4), 0, live(i, t, 3))
                    if live(i, t, 2):
                        project_v(*lagged(i, t, 2), j, fed, before[j])
                if live(i, t, 4):
                    turn_o(*lagged(i, t, 4), 1, live(i, t, 3))
                if live(i, t, 3):
                    if ffn and t >= 1:
                        wait(pe, gtd, 3 * (i - 2) + t)
                    else:
                        wait(pe, onorm, 2 * (g - 4) + 2)
                    product(*lagged(i, t, 3), (0, 1))
                if live(i, t, 4):
                    if live(i, t, 2):
                        wait(pe, v_ev, 2 * (g - 2) + 1)
                    else:
                        wait(pe, resid, g - 4)
                    project_o(*lagged(i, t, 4), (0, 1))
                if live(i, t, 3):
                    product(*lagged(i, t, 3), (2,))
                if live(i, t, 4):
                    project_o(*lagged(i, t, 4), (2, 3))
                if live(i, t, -1):
                    if live(i, t, 2):
                        wait(pe, v_ev, 2 * (g - 2) + 2)
                    else:
                        wait(pe, rot, 4 * g + 4)
                    turn_x(*lagged(i, t, -1))
                if live(i, t, 3):
                    product(*lagged(i, t, 3), (3,))
                if live(i, t, 4):
                    project_o(*lagged(i, t, 4), (4, 5, 6, 7))
                if ffn and t == 3:
                    if live(i, t, -1):
                        pe.wait_ge(xt_ev, g + 2)
                    elif live(i, t, 2):
                        pe.wait_ge(v_ev, 2 * (g - 2) + 2)
                    else:
                        pe.wait_ge(xn_ev, i - 1)
                    contract(i - 2)

            pipeline(pe, slot)

        @block.scalar
        def _(act):
            act.wait_ge(cleared, 2)

            def copy_x(i, t):
                act.wait_ge(xt_mm, NT * i + t + 1)
                act.activation(xT[0:DH, t * P:(t + 1) * P], PJ[1][0:DH, 0:P], ACT.Copy)
                act.activation(xT[DH:P, t * P + 1:(t + 1) * P + 1], PJ[1][DH:P, 0:P], ACT.Copy).then_inc(xt_ev, 1)

            def square(i, t, j):
                g = NT * i + t
                act.wait_ge(qk_mm, 4 * g + j + 1)
                wait(act, ssqd, 2 * g - 1 + j // 2)
                act.activation(sq[:, j, :], PJ[j % 2][:, :], ACT.Square).then_inc(sq_ev, 1)

            def copy_qk(i, t, j):
                g = NT * i + t
                act.wait_ge(tr_mm, 4 * g + j + 1)
                if j == 0:
                    wait(act, s_mm, g - 1)
                src = TR[j % 2][:, :].rearrange("p (q n) -> p q n", q=4)
                q = 4 * (j % 2)
                if j < 2:
                    dst = qT[:, t % 2, q:q + 4, :]
                else:
                    dst = kT[:, q:q + 4, WIN + t * P:WIN + (t + 1) * P]
                act.activation(dst, src, ACT.Copy).then_inc(tr_ev, 1)

            def copy_p(i, t, j):
                g = NT * i + t
                act.wait_ge(pt_mm, 2 * g + j + 1)
                wait(act, o_mm, g)
                act.activation(pT[:, 4 * j:4 * j + 4, :], TR[j][:, :].rearrange("p (q n) -> p q n", q=4),
                               ACT.Copy).then_inc(pt_ev, 1)

            def copy_v(i, t, j):
                g = NT * i + t
                act.wait_ge(v_mm, 2 * g + j + 1)
                for back in (1, 2):
                    if live(i, t, back):
                        act.wait_ge(vp_ld[(t - back) % 2], vp_count(*lagged(i, t, back)))
                act.activation(v[:, t % 2, j, :], PJ[j][:, :], ACT.Copy).then_inc(v_ev, 1)

            def copy_o(i, t, j):
                g = NT * i + t
                act.wait_ge(ot_mm, 2 * g + j + 1)
                wait(act, wo_mm, g)
                act.activation(oT[:, 4 * j:4 * j + 4, :], TR[j][:, :].rearrange("p (q n) -> p q n", q=4),
                               ACT.Copy).then_inc(ot_ev, 1)

            def exponentials(i, t, e):
                g = NT * i + t
                act.wait_ge(subd, 2 * g + e + 1)
                row = pr[:, t % 2, :, e, :]
                act.activation(row, row, ACT.Exp).then_inc(p_exp, 1)

            def gelu(i, k):
                n = FCH[k][1]
                act.wait_ge(ga_mm, 3 * i + k + 1)
                wait(act, gtd, 3 * i + (k == 2))
                act.activation(gel[0:n, k % 2, :], OB[0][0:n, :], ACT.Gelu,
                               bias=WF[0:n, F_B1 + 3 + k:F_B1 + 4 + k]).then_inc(ge_ev, 1)

            def layernorm(i):
                act.wait_ge(lnc, LN_STEPS * i + LN_STEPS)
                for t in range(NT):
                    last = act.activation(xn[:, t, :], xs[:, t, :], ACT.Identity, bias=nmean[:, t:t + 1],
                                          scale=rn[:, 0, 2 * HEADS + t:2 * HEADS + t + 1])
                last.then_inc(xnd, 1)

            def copy_xn(i):
                wait(act, wf_ld, 16 * (i // NB))
                act.wait_ge(xn_mm, i + 1)
                act.activation(hT[:, :], PJ[1][:, :], ACT.Identity, scale=WF[:, F_LNG:F_LNG + 1],
                               bias=WF[:, F_LNB:F_LNB + 1]).then_inc(xn_ev, 1)

            def load_table(n, kind):
                wait(act, tables_in, 2 * n + kind)
                act.activation(one[:, 1 + kind:2 + kind], one[:, 0:1],
                               ACT.Exp if kind else ACT.Gelu).then_inc(tables_in, 1)

            copy_x(0, 0)

            def slot(i, t):
                for j in range(4):
                    if live(i):
                        square(i, t, j)
                    if j == 0 and live(i - 2) and t == 1:
                        copy_xn(i - 2)
                    if live(i, t, 1):
                        copy_qk(*lagged(i, t, 1), j)
                    if j == 2 and live(i - 2) and t >= 1:
                        gelu(i - 2, t - 1)
                for j in range(2):
                    if live(i, t, 3):
                        copy_p(*lagged(i, t, 3), j)
                    if j == 1 and live(i, t, 4):
                        copy_o(*lagged(i, t, 4), 0)
                    if live(i, t, 2):
                        copy_v(*lagged(i, t, 2), j)
                if live(i, t, 4):
                    copy_o(*lagged(i, t, 4), 1)
                if live(i, t, -1):
                    copy_x(*lagged(i, t, -1))
                if live(i - 2) and t >= 1:
                    load_table(3 * (i - 2) + t - 1, 1)
                if live(i, t, 2):
                    for e in range(2):
                        exponentials(*lagged(i, t, 2), e)
                if live(i - 2) and t == 0:
                    layernorm(i - 2)
                if live(i - 2) and t < 3:
                    load_table(3 * (i - 2) + t, 0)
            pipeline(act, slot)

        @block.vector
        def _(dve):
            def rotate(i, t, j):
                g = NT * i + t
                dve.wait_ge(sq_ev, 4 * g + j + 1)
                wait(dve, added, 4 * g + j - 1)
                kind = 2 * (j // 2)
                table = lambda k: cols(tab, i, TSZ, (4 * t + k) * DH, DH)
                bank = PJ[j % 2][:, :]
                dve.tensor_tensor(rotA[:, j % 2, :].rearrange("p (h d) -> p h d", d=DH),
                                  bank.rearrange("p (h d) -> p h d", d=DH),
                                  table(kind).unsqueeze(1).broadcast_to([P, 8, DH]), ALU.mult)
                swapped = bank.rearrange("p (h s d) -> p h s d", h=8, s=2)[:, :, ::-1, :]
                sin = table(kind + 1).rearrange("p (s d) -> p s d", s=2).unsqueeze(1).broadcast_to([P, 8, 2, DH // 2])
                dve.tensor_tensor(rotB[:, j % 2, :].rearrange("p (h s d) -> p h s d", h=8, s=2),
                                  swapped, sin, ALU.mult).then_inc(rot, 1)

            def sum_squares(i, t, part):
                g = NT * i + t
                if part == 0:
                    wait(dve, newt, RN_STEPS * (g - 1))
                dve.tensor_reduce(ssq[:, t % 2, HEADS * part:HEADS * (part + 1)],
                                  sq[:, 2 * part:2 * part + 2, :].rearrange("p j (h d) -> p (j h) d", d=DH),
                                  AX, ALU.add).then_inc(ssqd, 1)

            def inverse_norms(i, t):
                lo, hi = 0 if live(i) else 2 * HEADS, 2 * HEADS
                if live(i):
                    dve.wait_ge(ssqd, 2 * (NT * i + t) + 2)
                if live(i - 2) and t == 0:
                    moments(i - 2)
                    hi += NT
                s = ssq[:, t % 2, lo:hi]
                steps = [lambda: dve.tensor_scalar(s, s, 1e-24, None, ALU.max)]
                steps += rsqrt_steps(dve, s, rn[:, t, lo:hi], nt[:, 0, lo:hi], nt[:, 1, lo:hi])
                assert len(steps) == RN_STEPS
                before = NT * i + t if live(i) else TILES * DEPTH + i - BATCHES
                for k, make in enumerate(steps):
                    make().then_inc(newt, 1)
                    dve.wait_ge(newt, RN_STEPS * before + k + 1)
                if hi > 2 * HEADS:
                    dve.scalar_tensor_tensor(nmean[:, :], mv[:, :, 0], -1.0, rn[:, 0, 2 * HEADS:hi],
                                             ALU.mult, ALU.mult).then_inc(lnc, 1)

            def moments(i):
                dve.wait_ge(xs_ld, 48 * i + 48)
                wait(dve, xn_mm, i)
                for t in range(NT):
                    last = dve.bn_stats(stats[:, t, :], xs[:, t, :])
                last.then_inc(lnc, 1)
                wait_apart(dve, passed["dve"], lnc, LN_STEPS * i + 1)
                for t in range(NT):
                    last = dve.bn_aggr(mv[:, t, :], stats[:, t, :])
                last.then_inc(lnc, 1)
                dve.wait_ge(lnc, LN_STEPS * i + 2)
                dve.tensor_scalar(ssq[:, 0, 2 * HEADS:], mv[:, :, 1], EPS, None, ALU.add).then_inc(lnc, 1)
                dve.wait_ge(lnc, LN_STEPS * i + 3)

            def shift(i, t, e):
                g = NT * i + t
                dve.wait_ge(s_mm, g + 1)
                wait(dve, pt_mm, 2 * (g - 1))
                s = SC[e][:, :].rearrange("p (q k) -> p q k", q=PAIRS)
                dve.tensor_reduce(mx[:, e, :], s, AX, ALU.max).then_inc(mxd, 1)
                dve.wait_ge(mxd, 2 * g + e + 1)
                dve.tensor_tensor(pr[:, t % 2, :, e, :], s,
                                  mx[:, e, :].unsqueeze(2).broadcast_to([P, PAIRS, 2 * WIN]),
                                  ALU.subtract).then_inc(subd, 1)

            def row_sums(i, t):
                g = NT * i + t
                for e in range(2):
                    dve.wait_ge(p_exp, 2 * g + e + 1)
                    dve.tensor_reduce(rsum[:, e, :], pr[:, t % 2, :, e, :], AX, ALU.add).then_inc(sumd, 1)
                dve.wait_ge(sumd, 2 * g + 2)
                dve.reciprocal(rinv[:, :, :], rsum[:, :, :]).then_inc(invd, 1)

            def normalize_o(i, t):
                g = NT * i + t
                dve.wait_ge(o_mm, g + 1)
                dve.wait_ge(invd, g + 1)
                wait(dve, ot_mm, 2 * g)
                for e in range(2):
                    dve.tensor_tensor(o[:, :, e, :], OB[e][:, :].rearrange("p (q d) -> p q d", d=DH),
                                      rinv[:, e, :].unsqueeze(2).broadcast_to([P, PAIRS, DH]),
                                      ALU.mult).then_inc(onorm, 1)

            def add_attention(i, t):
                g = NT * i + t
                dve.wait_ge(wo_mm, g + 1)
                rows = y_cols(i, t * P, P)
                dve.tensor_tensor(rows, PJ[0][:, 0:P], rows, ALU.add).then_inc(resid, 1)

            def gate(i, k):
                n = FCH[k][1]
                dve.wait_ge(ge_ev, 3 * i + k + 1)
                if k == 0:
                    wait(dve, y2_mm, i)
                dve.scalar_tensor_tensor(gT[0:n, k, :], OB[1][0:n, :], WF[0:n, F_B1 + k:F_B1 + k + 1],
                                         gel[0:n, k % 2, :], ALU.add, ALU.mult).then_inc(gtd, 1)

            def add_ffn(i):
                dve.wait_ge(y2_mm, i + 1)
                rows = y_cols(i, 0, NTOK)
                dve.tensor_tensor(rows, PJ[1][:, :], rows, ALU.add).then_inc(yd, 1)

            dve.memset(kT[:, :, 0:WIN], 0.0)
            dve.memset(vp[:, :, 0, :], 0.0)
            dve.memset(xT[:, 0:1], 0.0)
            dve.memset(xs[0:1, 0, DH:P], 0.0).then_inc(cleared, 1)
            dve.wait_ge(cleared, 2)

            def slot(i, t):
                if live(i, t, 3):
                    row_sums(*lagged(i, t, 3))
                if live(i):
                    rotate(i, t, 0)
                    rotate(i, t, 1)
                if live(i, t, 2):
                    shift(*lagged(i, t, 2), 0)
                if live(i):
                    rotate(i, t, 2)
                    rotate(i, t, 3)
                if live(i - 2) and t >= 1:
                    gate(i - 2, t - 1)
                if live(i, t, 2):
                    shift(*lagged(i, t, 2), 1)
                if live(i):
                    sum_squares(i, t, 0)
                    sum_squares(i, t, 1)
                if live(i) or live(i - 2) and t == 0:
                    inverse_norms(i, t)
                if live(i, t, 3):
                    normalize_o(*lagged(i, t, 3))
                if live(i, t, 4):
                    add_attention(*lagged(i, t, 4))
                if live(i - 2) and t == 3:
                    add_ffn(i - 2)

            pipeline(dve, slot)

        @block.gpsimd
        def _(pool):
            def copy_y(i, t):
                g = NT * i + t
                if t == 0:
                    wait(pool, yd, i - NB + 1)
                wait_apart(pool, passed["pool"], xt_mm, g - 1)
                pool.tensor_copy(yc[:, t % 2, :], y_cols(i, t * P, P)).then_inc(ycd, 1)

            def add(i, t, j):
                g = NT * i + t
                pool.wait_ge(rot, 4 * g + j + 1)
                wait(pool, tr_mm, 4 * (g - 2) + j + 1)
                pool.tensor_tensor(qk[:, t % 2, j, :], rotA[:, j % 2, :], rotB[:, j % 2, :], ALU.add).then_inc(added, 1)

            def normalize(i, t, j):
                g = NT * i + t
                pool.wait_ge(newt, RN_STEPS * (g + 1))
                pool.wait_ge(added, 4 * g + j + 1)
                half = qk[:, t % 2, j, :].rearrange("p (h d) -> p h d", d=DH)
                scale = rn[:, t, 8 * j:8 * j + 8].unsqueeze(2).broadcast_to([P, 8, DH])
                pool.tensor_tensor(half, half, scale, ALU.mult).then_inc(normd, 1)

            pool.memset(next_WF[:, F_W2 + 2 * P:FSZ], 0.0)
            pool.memset(one[:, :], 0.0)
            pool.memset(gT[:, 2, :], 1.0).then_inc(cleared, 1)
            pool.wait_ge(cleared, 2)
            copy_y(0, 0)

            def layer(l):
                for n in range(TILES):
                    i, t = NB * l + n // NT, n % NT
                    if n < TILES - 1 or not (isinstance(l, int) and l == DEPTH - 1):
                        copy_y(*lagged(i, t, -1))
                    for j in range(4):
                        add(i, t, j)
                    for j in range(4):
                        normalize(i, t, j)
                    if n == 11 and not (isinstance(l, int) and l == DEPTH - 1):
                        pool.wait_ge(wa_ld, 16 * ATTN_DMAS * (l + 1))
                        build_tables(pool, tab, tab_base, W, tabs, (l + 1) % 2)

            layer(0)
            with pool.Fori(1, DEPTH - 1) as l:
                layer(l)
            layer(DEPTH - 1)

        @block.sync
        def _(sp):
            def move_v(i, t):
                g = NT * i + t
                wait_apart(sp, passed["sp"], v_ev, 2 * g + 2)
                wait_apart(sp, passed["sp"], o_mm, g - 1)
                dst, s = vp[:, t % 2], vp_ld[t % 2]
                for e in range(2):
                    at = DH * e
                    for w in range(1, NWIN):
                        sp.dma_start(dst[at:at + 2 * WIN, w, :],
                                     v[WIN * (w - 1):WIN * (w + 1), t % 2, e, :]).then_inc(s, 16)
                    sp.dma_start(dst[at + WIN:at + 2 * WIN, 0, :], v[0:WIN, t % 2, e, :]).then_inc(s, 16)
                    if t > 0:
                        sp.dma_start(dst[at:at + WIN, 0, :], v[P - WIN:P, 1 - t % 2, e, :]).then_inc(s, 16)

            def shift_y(i):
                wait_apart(sp, passed["sp"], resid, NT * i + NT)
                wait_apart(sp, passed["sp"], xnd, i)
                rows = lambda s: y_cols(i, 0, NTOK, s).rearrange("p (t n) -> p t n", n=P)
                sp.dma_start(xs[:, :, 0:DH], rows(slice(0, P))[:, :, 0:DH]).then_inc(xs_ld, 16)
                sp.dma_start(xs[1:P, :, DH:P], rows(slice(0, P - 1))[:, :, DH:P]).then_inc(xs_ld, 16)
                sp.dma_start(xs[0:1, 1:NT, DH:P], rows(slice(P - 1, P))[:, 0:NT - 1, DH:P]).then_inc(xs_ld, 16)

            sp.wait_ge(cleared, 2)
            move_v(0, 0)
            move_v(0, 1)

            def layer(l):
                final = isinstance(l, int) and l == DEPTH - 1
                for n in range(NB):
                    i = NB * l + n
                    if n == 1:
                        wait_apart(sp, passed["sp"], yd, i - 1)
                        if not (isinstance(l, int) and l == 0):
                            wait_apart(sp, passed["sp"], next_ld, 16 * FFN_DMAS * l)
                            sp.dma_start(WF[:, :], next_WF[:, :]).then_inc(wf_ld, 16)
                        if not final:
                            load_attn(sp, a, W, wa_ld, l + 1, (l + 1) % 2 * WSZ)
                    if n == 2 and not final:
                        wait_apart(sp, passed["sp"], wf_ld, 16 * l)
                        load_ffn(sp, a, next_WF, next_ld, l + 1)
                    move_v(i, 2)
                    move_v(i, 3)
                    if not (final and n == NB - 1):
                        move_v(i + 1, 0)
                        move_v(i + 1, 1)
                    shift_y(i)

            layer(0)
            with sp.Fori(1, DEPTH - 1) as l:
                layer(l)
            layer(DEPTH - 1)

    sum_ok, stored = sem("summed"), sem("out_stored")
    with nc.Block() as block:
        @block.sync
        def _(sp):
            for b in range(NB):
                sp.wait_ge(sum_ok, b + 1)
                sp.dma_start(out[b].rearrange("(t p) d -> p t d", p=P),
                             x[:, NT * b:NT * (b + 1), :]).then_inc(stored, 16)
            sp.wait_ge(stored, 16 * NB)

        @block.vector
        def _(dve):
            for b in range(NB):
                rows = x[:, NT * b:NT * (b + 1), :]
                dve.tensor_tensor(rows, rows, y[:, NTOK * b:NTOK * (b + 1)].rearrange("p (t n) -> p t n", n=P),
                                  ALU.add).then_inc(sum_ok, 1)


NAMES = ["L0_attn_" + n for n in (
    "x", "ln_g", "ln_b", "Wq", "Wkv", "null_kv", "null_attn_bias", "pb_w0", "pb_b0", "pb_ln0_g", "pb_ln0_b", "pb_w1",
    "pb_b1", "pb_ln1_g", "pb_ln1_b", "pb_w2", "pb_b2", "Wo", "out_ln_g", "out_ln_b")] + ["L0_ffn_" + n for n in (
    "Wqkv", "q_scale", "k_scale", "Wo", "ln_g", "ln_b", "W1", "b1", "W2", "b2")]


def kernel(**inputs):
    import concourse.bacc as _bacc
    from concourse.bass_utils import run_bass_kernel_spmd as _run

    nc = _bacc.Bacc("TRN2", target_bir_lowering=False, num_devices=1)
    arrays, args = {}, {}
    for name in NAMES:
        arr = np.ascontiguousarray(inputs[name])
        arrays[f"in_{name}"] = arr
        args[name] = nc.dram_tensor(f"in_{name}", arr.shape, mybir.dt.from_np(arr.dtype), kind="ExternalInput").ap()
    out = nc.dram_tensor("out_0", (NB, NTOK, P), F32, kind="ExternalOutput").ap()
    build(nc, args, out)
    r = _run(nc, [arrays], core_ids=[0])
    return r.results[0]["out_0"]
```
